# Optimizing a Trainium2 kernel written in Bass

```python
import numpy as np
import jax
import jax.numpy as jnp

def _softmax(x, axis=-1):
    return jax.nn.softmax(x, axis=axis)

def _gelu(x):
    return jax.nn.gelu(x, approximate=True)

def _silu(x):
    return jax.nn.silu(x)

def _sigmoid(x):
    return jax.nn.sigmoid(x)

def _layernorm(x, axis=-1, eps=1e-05):
    m = jnp.mean(x, axis=axis, keepdims=True)
    v = jnp.var(x, axis=axis, keepdims=True)
    return (x - m) / jnp.sqrt(v + eps)

def _scatter_add(tgt, idx, src, axis=0):
    return tgt.at[idx].add(src)

def _segment_sum(src, seg, n):
    return jax.ops.segment_sum(src, seg, n)
kernel_name = 'mk_flamingo_gated_d2_seqx_r8_e8e5f8'

def setup_inputs(seed: int=0):
    np.random.seed(seed)
    _w = jnp.asarray

    def _rec_inputs():
        import jax
        import jax.numpy as jnp
        _rk = jax.random.key(seed)
        x = -0.0002928 + 1 * jax.random.normal(jax.random.fold_in(_rk, 1), (16, 64, 128), jnp.float32)
        _lenS = 64 - jax.random.randint(jax.random.fold_in(_rk, 7), (16,), 0, max(1, 64 // 4) + 1, jnp.int32)
        _lenS2 = 64 - jax.random.randint(jax.random.fold_in(_rk, 8), (16,), 0, max(1, 64 // 4) + 1, jnp.int32)
        _ctx_1024P = jax.random.normal(jax.random.fold_in(_rk, 11), (16, 16, 128), jnp.float32)
        _ctx_1024c = jax.random.dirichlet(jax.random.fold_in(_rk, 511), 0.3 * jnp.ones((16,), jnp.float32), (16, 64))
        _ctx_1024t = jnp.einsum('bsk,bkd->bsd', _ctx_1024c, _ctx_1024P)
        _ctx_1024t = _ctx_1024t * jax.lax.rsqrt(jnp.mean(jnp.square(_ctx_1024t)) + 1e-12) * 0.953939
        ctx_1024 = -1.39393e-06 + 0.999914 * (_ctx_1024t + 0.3 * jax.random.normal(jax.random.fold_in(_rk, 611), (16, 64, 128), jnp.float32))
        _validS = jnp.arange(64)[None, :] < _lenS[:, None]
        _validS2 = jnp.arange(64)[None, :] < _lenS2[:, None]
        _causal = jnp.tril(jnp.ones((64, 64), dtype=bool))
        mask_BxS2_ff1 = jnp.where(jnp.ones((16, 64), dtype=bool), 1.0, 0.0).astype(jnp.float32)
        _g = jax.random.normal(jax.random.fold_in(_rk, 9001), (2, 2), jnp.float32)
        _g = jnp.sign(_g) * jnp.maximum(jnp.abs(_g), 1.0) + (_g == 0) * 1.0
        g_xattn = _g[0]
        g_ffn = _g[1]
        return (x, ctx_1024, mask_BxS2_ff1, g_xattn, g_ffn)
    x, ctx_1024, mask_BxS2_ff1, g_xattn, g_ffn = _rec_inputs()

    def _L0_xattn_setup():
        import jax, jax.numpy as jnp
        import numpy as np
        N, T, D_KQ, E_KQ, D_V, E_V, H = (2, 256, 128, 128, 128, 128, 16)

        def _shifted_causal_mask(T):
            row = jnp.arange(T)[:, None]
            col = jnp.arange(T)[None, :]
            mask = jnp.where(col < row, 0.0, -jnp.inf).astype(jnp.float32)
            return mask.at[0, 0].set(0.0)
        key = jax.random.key(seed)
        ks = jax.random.split(key, 12)

        def lin(k, fan_in, fan_out):
            return jax.random.normal(k, (fan_in, fan_out), jnp.float32) * (1.0 / np.sqrt(fan_in))
        return {'kq': jax.random.normal(ks[0], (N, T, D_KQ), jnp.float32), 'v': jax.random.normal(ks[1], (N, T, D_V), jnp.float32), 'Wk': lin(ks[2], D_KQ, E_KQ), 'bk': jnp.zeros((E_KQ,), jnp.float32), 'Wq': lin(ks[3], D_KQ, E_KQ), 'bq': jnp.zeros((E_KQ,), jnp.float32), 'Wv': lin(ks[4], D_V, E_V), 'bv': jnp.zeros((E_V,), jnp.float32), 'W1': lin(ks[5], E_V, 4 * E_V), 'b1': jnp.zeros((4 * E_V,), jnp.float32), 'W2': lin(ks[6], 4 * E_V, E_V), 'b2': jnp.zeros((E_V,), jnp.float32)}
    _L0_xattn_all = _L0_xattn_setup()
    _L0_xattn_in = {k: v for k, v in _L0_xattn_all.items() if k in ('Wk', 'bk', 'Wq', 'bq', 'Wv', 'bv', 'W1', 'b1', 'W2', 'b2')}
    del _L0_xattn_all

    def _L0_ffn_setup():
        import jax, jax.numpy as jnp
        import numpy as np
        GROUP = 16
        EPS = 1e-05

        def _dequant(q, scale):
            w = q.astype(jnp.float32) / 7.5 - 1.0
            return w * jnp.repeat(scale, GROUP, axis=1)

        def _qlora_linear(x, q, scale, bias, la, lb):
            w = _dequant(q, scale)
            base = jnp.einsum('btd,od->bto', x, w) + bias
            lora = jnp.einsum('btr,or->bto', jnp.einsum('btd,rd->btr', x, la), lb)
            return base + lora

        def _layernorm(x, g, b):
            mu = jnp.mean(x, axis=-1, keepdims=True)
            var = jnp.mean(jnp.square(x - mu), axis=-1, keepdims=True)
            return (x - mu) * jax.lax.rsqrt(var + EPS) * g + b
        key = jax.random.key(seed)
        ks = jax.random.split(key, 6)
        D, R, B, T = (128, 32, 8, 512)
        x = jax.random.normal(ks[0], (B, T, D), dtype=jnp.float32)
        qweights = jax.random.randint(ks[1], (6, D, D), 0, 16, dtype=jnp.int32)
        scales = jax.random.uniform(ks[2], (6, D, D // GROUP), dtype=jnp.float32)
        biases = jax.random.normal(ks[3], (6, D), dtype=jnp.float32) * 0.02
        lora_a = jax.random.normal(ks[4], (6, R, D), dtype=jnp.float32) * 0.02
        lora_b = jax.random.normal(ks[5], (6, D, R), dtype=jnp.float32) * 0.02
        ln_gamma = jnp.ones((3, D), dtype=jnp.float32)
        ln_beta = jnp.zeros((3, D), dtype=jnp.float32)
        return {'x': x, 'qweights': qweights, 'scales': scales, 'biases': biases, 'lora_a': lora_a, 'lora_b': lora_b, 'ln_gamma': ln_gamma, 'ln_beta': ln_beta}
    _L0_ffn_all = _L0_ffn_setup()
    _L0_ffn_in = {k: v for k, v in _L0_ffn_all.items() if k in ('qweights', 'scales', 'biases', 'lora_a', 'lora_b', 'ln_gamma', 'ln_beta')}
    del _L0_ffn_all

    def _L1_xattn_setup():
        import jax, jax.numpy as jnp
        import numpy as np
        D_MODEL = 128
        HEADS = 16
        DEPTH = D_MODEL // HEADS
        B, S = (4, 512)
        EPS_K = 1e-06
        EPS_LN = 1e-06

        def _layernorm(x, g, b):
            m = jnp.mean(x, axis=-1, keepdims=True)
            var = jnp.var(x, axis=-1, keepdims=True)
            return (x - m) * jax.lax.rsqrt(var + EPS_LN) * g + b

        def _split_heads(x):
            bsz, sl, _ = x.shape
            return x.reshape(bsz, sl, HEADS, DEPTH).transpose(0, 2, 1, 3)
        key = jax.random.key(seed)
        ks = jax.random.split(key, 8)
        lecun = 1.0 / np.sqrt(D_MODEL)
        glorot = np.sqrt(2.0 / (D_MODEL + D_MODEL))
        return {'q': jax.random.normal(ks[0], (B, S, D_MODEL), jnp.float32), 'k': jax.random.normal(ks[1], (B, S, D_MODEL), jnp.float32), 'v': jax.random.normal(ks[2], (B, S, D_MODEL), jnp.float32), 'mask': jnp.ones((B, S), jnp.float32), 'wq': jax.random.normal(ks[3], (D_MODEL, D_MODEL), jnp.float32) * lecun, 'wk': jax.random.normal(ks[4], (D_MODEL, D_MODEL), jnp.float32) * lecun, 'wv': jax.random.normal(ks[5], (D_MODEL, D_MODEL), jnp.float32) * lecun, 'ln_gamma': jnp.ones((D_MODEL,), jnp.float32), 'ln_beta': jnp.zeros((D_MODEL,), jnp.float32), 'dense_w': jax.random.normal(ks[6], (D_MODEL, D_MODEL), jnp.float32) * glorot, 'dense_b': jnp.zeros((D_MODEL,), jnp.float32)}
    _L1_xattn_all = _L1_xattn_setup()
    _L1_xattn_in = {k: v for k, v in _L1_xattn_all.items() if k in ('wq', 'wk', 'wv', 'ln_gamma', 'ln_beta', 'dense_w', 'dense_b')}
    del _L1_xattn_all

    def _L1_ffn_setup():
        import jax, jax.numpy as jnp
        import numpy as np
        HIDDEN = 128
        INTER = 352
        N_EXPERTS = 8
        TOP_K = 2
        key = jax.random.key(seed)
        k1, k2, k3, k4 = jax.random.split(key, 4)
        hidden_states = jax.random.normal(k1, (4, 256, HIDDEN), dtype=jnp.float32)
        gate_w = jax.random.normal(k2, (N_EXPERTS, HIDDEN), dtype=jnp.float32) * HIDDEN ** (-0.5)
        w1_stacked = jax.random.normal(k3, (N_EXPERTS, HIDDEN, 2 * INTER), dtype=jnp.float32) * HIDDEN ** (-0.5)
        w2_stacked = jax.random.normal(k4, (N_EXPERTS, INTER, HIDDEN), dtype=jnp.float32) * INTER ** (-0.5)
        return {'hidden_states': hidden_states, 'gate_w': gate_w, 'w1_stacked': w1_stacked, 'w2_stacked': w2_stacked}
    _L1_ffn_all = _L1_ffn_setup()
    _L1_ffn_in = {k: v for k, v in _L1_ffn_all.items() if k in ('gate_w', 'w1_stacked', 'w2_stacked')}
    del _L1_ffn_all
    return {'x': x, 'ctx_1024': ctx_1024, 'mask_BxS2_ff1': mask_BxS2_ff1, 'g_xattn': g_xattn, 'g_ffn': g_ffn, 'L0_xattn_Wk': _L0_xattn_in['Wk'], 'L0_xattn_bk': _L0_xattn_in['bk'], 'L0_xattn_Wq': _L0_xattn_in['Wq'], 'L0_xattn_bq': _L0_xattn_in['bq'], 'L0_xattn_Wv': _L0_xattn_in['Wv'], 'L0_xattn_bv': _L0_xattn_in['bv'], 'L0_xattn_W1': _L0_xattn_in['W1'], 'L0_xattn_b1': _L0_xattn_in['b1'], 'L0_xattn_W2': _L0_xattn_in['W2'], 'L0_xattn_b2': _L0_xattn_in['b2'], 'L0_ffn_qweights': _L0_ffn_in['qweights'], 'L0_ffn_scales': _L0_ffn_in['scales'], 'L0_ffn_biases': _L0_ffn_in['biases'], 'L0_ffn_lora_a': _L0_ffn_in['lora_a'], 'L0_ffn_lora_b': _L0_ffn_in['lora_b'], 'L0_ffn_ln_gamma': _L0_ffn_in['ln_gamma'], 'L0_ffn_ln_beta': _L0_ffn_in['ln_beta'], 'L1_xattn_wq': _L1_xattn_in['wq'], 'L1_xattn_wk': _L1_xattn_in['wk'], 'L1_xattn_wv': _L1_xattn_in['wv'], 'L1_xattn_ln_gamma': _L1_xattn_in['ln_gamma'], 'L1_xattn_ln_beta': _L1_xattn_in['ln_beta'], 'L1_xattn_dense_w': _L1_xattn_in['dense_w'], 'L1_xattn_dense_b': _L1_xattn_in['dense_b'], 'L1_ffn_gate_w': _L1_ffn_in['gate_w'], 'L1_ffn_w1_stacked': _L1_ffn_in['w1_stacked'], 'L1_ffn_w2_stacked': _L1_ffn_in['w2_stacked']}

def reference(x, ctx_1024, mask_BxS2_ff1, g_xattn, g_ffn, L0_xattn_Wk, L0_xattn_bk, L0_xattn_Wq, L0_xattn_bq, L0_xattn_Wv, L0_xattn_bv, L0_xattn_W1, L0_xattn_b1, L0_xattn_W2, L0_xattn_b2, L0_ffn_qweights, L0_ffn_scales, L0_ffn_biases, L0_ffn_lora_a, L0_ffn_lora_b, L0_ffn_ln_gamma, L0_ffn_ln_beta, L1_xattn_wq, L1_xattn_wk, L1_xattn_wv, L1_xattn_ln_gamma, L1_xattn_ln_beta, L1_xattn_dense_w, L1_xattn_dense_b, L1_ffn_gate_w, L1_ffn_w1_stacked, L1_ffn_w2_stacked):
    import jax
    import jax.numpy as jnp

    def _L0_xattn_ref(kq, v, Wk, bk, Wq, bq, Wv, bv, W1, b1, W2, b2):
        import jax, jax.numpy as jnp
        import numpy as np
        N, T, D_KQ, E_KQ, D_V, E_V, H = (2, 256, 128, 128, 128, 128, 16)

        def _shifted_causal_mask(T):
            row = jnp.arange(T)[:, None]
            col = jnp.arange(T)[None, :]
            mask = jnp.where(col < row, 0.0, -jnp.inf).astype(jnp.float32)
            return mask.at[0, 0].set(0.0)
        n, T, _ = kq.shape
        hd_kq = E_KQ // H
        hd_v = E_V // H
        k = (kq @ Wk + bk).reshape(n, T, H, hd_kq).transpose(0, 2, 1, 3)
        q = (kq @ Wq + bq).reshape(n, T, H, hd_kq).transpose(0, 2, 1, 3)
        vv = (v @ Wv + bv).reshape(n, T, H, hd_v).transpose(0, 2, 1, 3)
        scores = jnp.einsum('bhqd,bhkd->bhqk', q, k) + _shifted_causal_mask(T)
        attn = jax.nn.softmax(scores, axis=-1)
        out = jnp.einsum('bhqk,bhkd->bhqd', attn, vv)
        out = out.transpose(0, 2, 1, 3).reshape(n, T, E_V)
        h = jax.nn.gelu(out @ W1 + b1, approximate=False)
        return h @ W2 + b2

    def _L0_ffn_ref(x, qweights, scales, biases, lora_a, lora_b, ln_gamma, ln_beta):
        import jax, jax.numpy as jnp
        import numpy as np
        GROUP = 16
        EPS = 1e-05

        def _dequant(q, scale):
            w = q.astype(jnp.float32) / 7.5 - 1.0
            return w * jnp.repeat(scale, GROUP, axis=1)

        def _qlora_linear(x, q, scale, bias, la, lb):
            w = _dequant(q, scale)
            base = jnp.einsum('btd,od->bto', x, w) + bias
            lora = jnp.einsum('btr,or->bto', jnp.einsum('btd,rd->btr', x, la), lb)
            return base + lora

        def _layernorm(x, g, b):
            mu = jnp.mean(x, axis=-1, keepdims=True)
            var = jnp.mean(jnp.square(x - mu), axis=-1, keepdims=True)
            return (x - mu) * jax.lax.rsqrt(var + EPS) * g + b
        h = x
        for blk in range(3):
            i0, i1 = (2 * blk, 2 * blk + 1)
            y = _qlora_linear(h, qweights[i0], scales[i0], biases[i0], lora_a[i0], lora_b[i0])
            y = _layernorm(y, ln_gamma[blk], ln_beta[blk])
            y = jax.nn.gelu(y, approximate=False)
            y = _qlora_linear(y, qweights[i1], scales[i1], biases[i1], lora_a[i1], lora_b[i1])
            h = y + h
        return h

    def _L1_xattn_ref(q, k, v, mask, wq, wk, wv, ln_gamma, ln_beta, dense_w, dense_b):
        import jax, jax.numpy as jnp
        import numpy as np
        D_MODEL = 128
        HEADS = 16
        DEPTH = D_MODEL // HEADS
        B, S = (4, 512)
        EPS_K = 1e-06
        EPS_LN = 1e-06

        def _layernorm(x, g, b):
            m = jnp.mean(x, axis=-1, keepdims=True)
            var = jnp.var(x, axis=-1, keepdims=True)
            return (x - m) * jax.lax.rsqrt(var + EPS_LN) * g + b

        def _split_heads(x):
            bsz, sl, _ = x.shape
            return x.reshape(bsz, sl, HEADS, DEPTH).transpose(0, 2, 1, 3)
        bsz = q.shape[0]
        em = mask[:, None, :, None]
        qh = _split_heads(_layernorm(q @ wq, ln_gamma, ln_beta))
        kh = _split_heads(_layernorm(k @ wk, ln_gamma, ln_beta))
        vh = _split_heads(_layernorm(v @ wv, ln_gamma, ln_beta))
        q_prime = jax.nn.relu(qh) + EPS_K
        k_prime = (jax.nn.relu(kh) + EPS_K) * em
        vh = vh * em
        kv = jnp.einsum('bhnd,bhne->bhde', k_prime, vh)
        z = 1.0 / (jnp.einsum('bhnd,bhd->bhn', q_prime, k_prime.sum(axis=-2)) + EPS_K)
        att = jnp.einsum('bhnd,bhde,bhn->bhne', q_prime, kv, z)
        att = att.reshape(bsz, -1, D_MODEL)
        out = att @ dense_w + dense_b
        return _layernorm(out, ln_gamma, ln_beta)

    def _L1_ffn_ref(hidden_states, gate_w, w1_stacked, w2_stacked):
        import jax, jax.numpy as jnp
        import numpy as np
        HIDDEN = 128
        INTER = 352
        N_EXPERTS = 8
        TOP_K = 2
        B, S, H = hidden_states.shape
        x = hidden_states.reshape(-1, H)
        logits = x @ gate_w.T
        probs = jax.nn.softmax(logits, axis=-1)
        top_w, top_i = jax.lax.top_k(probs, TOP_K)
        top_w = top_w / jnp.sum(top_w, axis=-1, keepdims=True)
        E = w1_stacked.shape[0]
        I = w2_stacked.shape[1]
        out = jnp.zeros_like(x)
        for e in range(E):
            h = x @ w1_stacked[e]
            act = jax.nn.silu(h[:, :I]) * h[:, I:]
            oe = act @ w2_stacked[e]
            we = jnp.sum(jnp.where(top_i == e, top_w, 0.0), axis=-1)
            out = out + we[:, None] * oe
        return out.reshape(B, S, H)
    x = x + jnp.tanh(g_xattn[0]) * _L0_xattn_ref(_layernorm(x, axis=-1), ctx_1024, L0_xattn_Wk, L0_xattn_bk, L0_xattn_Wq, L0_xattn_bq, L0_xattn_Wv, L0_xattn_bv, L0_xattn_W1, L0_xattn_b1, L0_xattn_W2, L0_xattn_b2)
    x = x + jnp.tanh(g_ffn[0]) * _L0_ffn_ref(_layernorm(x, axis=-1), L0_ffn_qweights, L0_ffn_scales, L0_ffn_biases, L0_ffn_lora_a, L0_ffn_lora_b, L0_ffn_ln_gamma, L0_ffn_ln_beta)
    x = x + jnp.tanh(g_xattn[1]) * _L1_xattn_ref(_layernorm(x, axis=-1), ctx_1024, ctx_1024, mask_BxS2_ff1, L1_xattn_wq, L1_xattn_wk, L1_xattn_wv, L1_xattn_ln_gamma, L1_xattn_ln_beta, L1_xattn_dense_w, L1_xattn_dense_b)
    x = x + jnp.tanh(g_ffn[1]) * _L1_ffn_ref(_layernorm(x, axis=-1), L1_ffn_gate_w, L1_ffn_w1_stacked, L1_ffn_w2_stacked)
    return x

_drawn_inputs = setup_inputs


def setup_inputs(seed=0):
    import zlib

    import numpy as np

    out = dict(_drawn_inputs(seed))
    spreads = {'g_ffn': (-1.0, 0.6),
     'L0_xattn_bk': (0.0, 0.8),
     'L0_xattn_bq': (0.0, 0.1),
     'L0_xattn_bv': (0.0, 0.1),
     'L0_xattn_b1': (0.0, 0.1),
     'L0_xattn_b2': (0.0, 0.1),
     'L0_ffn_ln_gamma': (1.0, 0.2),
     'L0_ffn_ln_beta': (0.0, 0.1),
     'L1_xattn_ln_gamma': (1.0, 0.2),
     'L1_xattn_ln_beta': (0.0, 0.1),
     'L1_xattn_dense_b': (0.0, 0.1)}
    factors = {'L0_ffn_biases': 4.122, 'L0_ffn_lora_a': 4.204, 'L0_ffn_lora_b': 4.248}
    for name, (base, spread) in spreads.items():
        noise = np.random.default_rng([zlib.crc32(name.encode()), seed]).standard_normal(out[name].shape)
        drawn = base * np.exp(spread * noise) if base else spread * noise
        out[name] = jnp.asarray(drawn.astype(out[name].dtype))
    for name, factor in factors.items():
        out[name] = (out[name] * factor).astype(out[name].dtype)
    return out
```

```python
from contextlib import ExitStack

import concourse.bass as bass
from concourse import mybir

ALU = mybir.AluOpType
ACT = mybir.ActivationFunctionType
AX = mybir.AxisListType
F32 = mybir.dt.float32
BF16 = mybir.dt.bfloat16
I32 = mybir.dt.int32
U32 = mybir.dt.uint32

D = 128
S = 64
T = 8
HT = 4
HALF = 512
NH = 16
HD = 8
E = 8
INTER = 352
KC = [(0, 128), (128, 128), (256, 96)]
NEG = -1.0e30

R_BK, R_BQ, R_BV, R_B1, R_FB, R_FG, R_FBETA, R_LG, R_LB, R_GATE, R_MASK, R_END = 0, 1, 2, 3, 7, 13, 16, 19, 20, 21, 29, 37


def kv_batches(g):
    return [2 * m + g % 2 for m in range(3 * (g // 2), min(3 * (g // 2) + 3, 8))]


def flamingo(nc, x, ctx_in, mask, g_xattn, g_ffn, Wk, bk, Wq, bq, Wv, bv, W1, b1, W2, b2,
             qw, scales, fbias, lora_a, lora_b, ln_g, ln_b, wq1, wk1, wv1, lg1, lb1,
             dense_w, dense_b, gate_w, w1s, w2s, out):
    with ExitStack() as ctx:
        def sb(name, shape, dt=F32):
            return ctx.enter_context(nc.sbuf_tensor(name, shape, dt))

        def sem(name):
            return ctx.enter_context(nc.semaphore(name))

        ps = ctx.enter_context(nc.psum_tensor("ps", [128, 8, 512], F32))

        X = sb("X", [128, T, D])
        CX = sb("CX", [128, T, D])
        PR = sb("PR", [R_END, 128])
        PC = sb("PC", [128, R_END])
        wkqv = sb("wkqv", [128, 3, D])
        w1_sb = sb("w1_sb", [128, 4, D])
        w2_sb = sb("w2_sb", [128, 4, D])
        rows = sb("rows", [1, 8, D])
        bcast = sb("bcast", [128, 2, D])
        gts = sb("gts", [128, 4])
        tg = sb("tg", [128, 4])
        qw_sb = sb("qw_sb", [128, 6, D], I32)
        sc_sb = sb("sc_sb", [128, 6, 8])
        la_sb = sb("la_sb", [32, 6, D])
        lb_sb = sb("lb_sb", [128, 6, 32])
        wqkv1 = sb("wqkv1", [128, 3, D])
        dw_sb = sb("dw_sb", [128, D])
        ew1 = sb("ew1", [128, 2, 2 * INTER])
        ew2 = sb("ew2", [128, 2, 3, D])

        ident = sb("ident", [128, 128])
        identb = sb("identb", [128, 128], BF16)
        causal = sb("causal", [128, 8, S], BF16)
        hm = sb("hm", [128, NH])
        hmT = sb("hmT", [NH, 128])
        blk = sb("blk", [128, NH, HD])
        par = sb("par", [128, NH, HD])
        pairsel = sb("pairsel", [128, 4])
        neghalf = sb("neghalf", [128, HT])
        ones = sb("ones", [1, 128])
        iota8 = sb("iota8", [128, 8])

        XN = sb("XN", [128, T, D])
        XT = sb("XT", [128, 2, HALF])
        CT = sb("CT", [128, 2, HALF])
        kT = sb("kT", [128, 2, HALF])
        qT = sb("qT", [128, 2, HALF])
        Km = sb("Km", [128, NH, 2 * HALF])
        Vm = sb("Vm", [128, 16, D])
        P = sb("P", [128, 2, NH, S])
        PT = sb("PT", [128, 2, 8, 128])
        mx = sb("mx", [128, 2, NH])
        sm = sb("sm", [128, 2, NH])
        rc = sb("rc", [128, 2, NH])
        rT = sb("rT", [NH, 256])
        o0 = sb("o0", [128, 4, S])
        o1 = sb("o1", [128, 4, S])
        o2 = sb("o2", [128, 4, S])
        AT = sb("AT", [128, 2, HALF])
        hE = P[0:64].rearrange("p a h s -> p (a h s)").rearrange("p (f n e) -> p f n e", f=2, e=HD)
        H1 = sb("H1", [128, 4, HALF])
        wdq = sb("wdq", [128, 6, D])
        wf = H1[:].rearrange("p c (a d) -> p (c a) d", d=D)[:, 0:6, :]
        lbT = sb("lbT", [32, 6, D])
        weT = sb("weT", [128, 6, D])
        hT = sb("hT", [128, 2, HALF])
        YN = sb("YN", [128, T, D])
        gT = AT
        kp = sb("kp", [128, T, D])
        vx = sb("vx", [128, T, 132])
        kvx = sb("kvx", [128, 16, 144])
        zz = sb("zz", [128, 4, 2, NH])
        AO = CX
        kn, vn = AO, YN
        bst = sb("bst", [128, HT, 6])
        NLN = 22
        mv = sb("mv", [128, NLN, HT, 2])
        ve = sb("ve", [128, NLN, HT])
        rstd = sb("rstd", [128, NLN, HT])
        lg = sb("lg", [128, T, 8])
        top = sb("top", [128, T, 8])
        topi = sb("topi", [128, T, 8], U32)
        topf = sb("topf", [128, T, 8])
        dl = sb("dl", [128, T])
        el = sb("el", [128, T])
        den = sb("den", [128, T])
        tw = sb("tw", [128, T, 2])
        oh = sb("oh", [128, 2, T, 8])
        wexp = sb("wexp", [128, T, 8])
        wcur = sb("wcur", [128, 4, HT])
        sg = Km[:, 0:3, 0:HALF]
        am = Km[:, 3:6, 0:HALF]

        names = ["x", "ctx", "pr", "wkqv", "mlp", "rows", "gates", "q", "l1", "kmask"]
        ld = {n: sem("ld_" + n) for n in names}
        ld_e = [sem("ld_expert_even"), sem("ld_expert_odd")]
        stored = sem("stored")
        consts = sem("consts_ready")
        pool_step = sem("pool_step")
        dve_step = sem("dve_step")
        F = {n: sem("pe_" + n) for n in [
            "params", "ctxT", "v", "x1T", "k", "q", "lbT", "weT", "k1", "v1", "kv", "scores", "probsT", "heads",
            "recT", "rec", "up", "down", "x2T", "y", "yT", "z", "x3T", "q1", "q1T", "att", "hE", "attT", "dense",
            "x4T", "gate", "h0", "h1", "h2", "oe"]}
        M = {n: sem(n) for n in [
            "params_sb", "ctxT_sb", "vm_sb", "x1", "x1T_sb", "k_sb", "q_sb", "wdq_sb", "lbT_sb", "weT_sb",
            "k1_read", "v1_read", "kp_sb", "vx_sb", "kvx_sb", "centered", "exped", "rowmax", "sums", "probsT_sb", "recT_sb",
            "heads_sb", "AT_sb", "up_sb", "X1", "x2", "x2T_sb", "y_read", "yn", "gT_sb", "z_sb", "X2", "x3",
            "x3T_sb", "q1_read", "q1T_sb", "relu_sb", "att_sb", "hE_sb", "attT_sb", "dense_read", "X3", "x4", "x4T_sb", "gate_read",
            "dlog", "el_sb", "wexp_sb", "silu", "act_sb", "oe_read", "tanh_sb", "X4",
            "ln_var", "ln_rstd", "km_zero"]}

        block = ctx.enter_context(nc.Block())

        @block.sync
        def _(sp):
            sp.dma_start(X[:], x.rearrange("(t b) s d -> (b s) t d", b=2)).then_inc(ld["x"], 16)
            sp.dma_start(CX[:], ctx_in.rearrange("(t b) s d -> (b s) t d", b=2)).then_inc(ld["ctx"], 16)
            row = lambda a: a.rearrange("(a d) -> a d", d=128)
            stack = [(R_BK, 1, row(bk)), (R_BQ, 1, row(bq)), (R_BV, 1, row(bv)), (R_B1, 4, row(b1)),
                     (R_FB, 6, fbias), (R_FG, 3, ln_g), (R_FBETA, 3, ln_b), (R_LG, 1, row(lg1)),
                     (R_LB, 1, row(lb1)), (R_GATE, 8, gate_w), (R_MASK, 8, mask.rearrange("(t b) s -> t (b s)", b=2))]
            for r, n, src in stack:
                sp.dma_start(PR[r:r + n, :], src).then_inc(ld["pr"], 16)
            for i, w in enumerate((Wk, Wq, Wv)):
                sp.dma_start(wkqv[:, i, :], w).then_inc(ld["wkqv"], 16)
            sp.dma_start(w1_sb[:].rearrange("p c d -> p (c d)"), W1).then_inc(ld["mlp"], 16)
            sp.dma_start(w2_sb[:], W2.rearrange("(c p) d -> p c d", p=128)).then_inc(ld["mlp"], 16)
            sp.dma_start(qw_sb[:], qw.rearrange("n o d -> o n d")).then_inc(ld["q"], 16)
            sp.dma_start(sc_sb[:], scales.rearrange("n o g -> o n g")).then_inc(ld["q"], 16)
            sp.dma_start(la_sb[:], lora_a.rearrange("n r d -> r n d")).then_inc(ld["q"], 16)
            sp.dma_start(lb_sb[:], lora_b.rearrange("n o r -> o n r")).then_inc(ld["q"], 16)
            sp.dma_start(rows[:, 0, :], row(b2)).then_inc(ld["rows"], 16)
            for j, n in enumerate((0, 2, 4, 5)):
                sp.dma_start(rows[:, 1 + j, :], fbias[n:n + 1, :]).then_inc(ld["rows"], 16)
            sp.dma_start(rows[:, 5, :], row(dense_b)).then_inc(ld["rows"], 16)
            sp.dma_start(bcast[:, 0, :], lg1.partition_broadcast(128)).then_inc(ld["rows"], 16)
            sp.dma_start(bcast[:, 1, :], lb1.partition_broadcast(128)).then_inc(ld["rows"], 16)
            sp.dma_start(gts[:, 0:2], g_xattn.partition_broadcast(128)).then_inc(ld["gates"], 16)
            sp.dma_start(gts[:, 2:4], g_ffn.partition_broadcast(128)).then_inc(ld["gates"], 16)
            for i, w in enumerate((wq1, wk1, wv1)):
                sp.dma_start(wqkv1[:, i, :], w).then_inc(ld["l1"], 16)
            sp.dma_start(dw_sb[:], dense_w).then_inc(ld["l1"], 16)

            sp.wait_ge(M["km_zero"], 1)
            for hf in range(2):
                sp.wait_ge(M["k_sb"], hf + 1)
                for h in range(NH):
                    sp.dma_start(Km[HD * h:HD * h + HD, h, HALF * hf:HALF * hf + HALF],
                                 kT[HD * h:HD * h + HD, hf, :]).then_inc(ld["kmask"], 16)

            def load_expert(e, slot):
                sp.dma_start(ew1[:, slot, :], w1s[e]).then_inc(ld_e[slot], 16)
                w2e = w2s[e]
                sp.dma_start(ew2[:, slot, 0:2, :], w2e[0:256, :].rearrange("(c p) d -> p c d", p=128)).then_inc(ld_e[slot], 16)
                sp.dma_start(ew2[0:96, slot, 2, :], w2e[256:352, :]).then_inc(ld_e[slot], 16)

            load_expert(0, 0)
            load_expert(1, 1)
            with sp.Fori(1, E // 2) as i:
                for slot in range(2):
                    sp.wait_ge(F["oe"], 4 * i + 2 * slot - 2)
                    load_expert(2 * i + slot, slot)
            sp.wait_ge(M["X4"], 1)
            sp.dma_start(out.rearrange("(t b) s d -> (b s) t d", b=2), X[:]).then_inc(stored, 16)
            sp.wait_ge(stored, 16)

        @block.gpsimd
        def _(pool):
            g = nc.gpsimd
            n = [0]

            def link(ins):
                n[0] += 1
                ins.then_inc(pool_step, 1)
                pool.wait_ge(pool_step, n[0])

            g.memset(neghalf[:], -0.5)
            g.memset(ones[:], 1.0)
            g.memset(vx[:], 1.0)
            g.memset(hm[:], 1.0)
            g.memset(hmT[:], 1.0)
            g.memset(causal[:], 0.0)
            g.memset(par[:], 1.0)
            g.memset(ident[:], 0.0)
            link(g.memset(identb[:], 0.0))
            for t in (ident, identb):
                g.affine_select(out=t[:], in_=t[:], compare_op=ALU.not_equal, fill=1.0, base=0,
                                pattern=[[-1, 128]], channel_multiplier=1)
            g.iota(iota8[:], [[1, 8]], base=0, channel_multiplier=0, allow_small_or_imprecise_dtypes=True)
            link(g.affine_select(out=hm[:], in_=hm[:], compare_op=ALU.is_ge, fill=0.0, base=0,
                                 pattern=[[-HD, NH]], channel_multiplier=1))
            link(g.affine_select(out=hm[:], in_=hm[:], compare_op=ALU.is_ge, fill=0.0, base=HD - 1,
                                 pattern=[[HD, NH]], channel_multiplier=-1))
            link(g.affine_select(out=hmT[:], in_=hmT[:], compare_op=ALU.is_ge, fill=0.0, base=0,
                                 pattern=[[1, 128]], channel_multiplier=-HD))
            link(g.affine_select(out=hmT[:], in_=hmT[:], compare_op=ALU.is_ge, fill=0.0, base=HD - 1,
                                 pattern=[[-1, 128]], channel_multiplier=HD))
            for b in range(2):
                c = causal[64 * b:64 * b + 64, :, :]
                link(g.affine_select(out=c, in_=c, compare_op=ALU.is_gt, fill=NEG, base=0,
                                     pattern=[[0, 8], [-1, S]], channel_multiplier=1))
                link(g.memset(causal[64 * b:64 * b + 1, :, 0:1], 0.0))
            pv = par[:].rearrange("p (g two) d -> p g two d", two=2)
            link(g.memset(pv[0:64, :, 1, :], 0.0))
            g.memset(pv[64:128, :, 0, :], 0.0).then_inc(consts, 1)
            pool.wait_ge(consts, 1)
            for i in range(NLN):
                if i == 2:
                    for h in range(NH):
                        last = g.memset(Km[:, h, :], 0.0)
                    last.then_inc(M["km_zero"], 1)
                pool.wait_ge(M["ln_var"], i + 1)
                eps = 1e-6 if i in LN_1E6 else 1e-5
                link(g.tensor_scalar(ve[:, i, :], mv[:, i, :, 1], eps, 1.0, ALU.add, ALU.mult))
                g.tensor_tensor(rstd[:, i, :], ve[:, i, :], neghalf[:], ALU.pow).then_inc(M["ln_rstd"], 1)

        @block.tensor
        def _(pe):
            def transposes(bank, src, out_sem, n=HT):
                for t in range(n):
                    last = pe.transpose(ps[:, bank, 128 * t:128 * t + 128], src[:, t, :], ident[:])
                last.then_inc(out_sem, 1)

            def tokens_out(bank, srcT, weights, bias_row=None, extra=()):
                for t in range(HT):
                    o = ps[:, bank, 128 * t:128 * t + 128]
                    pairs = [(srcT[:, 128 * t:128 * t + 128], weights)] + [(a[:, 128 * t:128 * t + 128], b) for a, b in extra]
                    if bias_row is not None:
                        pairs.append((ones[:], bias_row))
                    for k, (l, r) in enumerate(pairs):
                        last = pe.matmul(o, l, r, start=(k == 0), stop=(k == len(pairs) - 1))
                return last

            pe.wait_ge(consts, 1)
            pe.wait_ge(ld["pr"], 16 * 11)
            pe.transpose(ps[:, 0, 0:R_END], PR[:, :], ident[0:R_END, 0:R_END]).then_inc(F["params"], 1)
            pe.wait_ge(ld["ctx"], 16)
            for hf in range(2):
                transposes(1 + hf, CX[:, HT * hf:HT * hf + HT, :], F["ctxT"])
            pe.wait_ge(ld["wkqv"], 48)
            for c in range(4):
                if c % 2 == 0:
                    pe.wait_ge(M["ctxT_sb"], c // 2 + 1)
                for b in range(4):
                    src = CT[:, c // 2, (4 * (c % 2) + b) * S:(4 * (c % 2) + b) * S + S]
                    for dup in range(2):
                        last = pe.matmul(ps[64 * dup:64 * dup + 64, 3 + c, 128 * b:128 * b + 128], src, wkqv[:, 2, :],
                                         start=True, stop=True)
                last.then_inc(F["v"], 1)
            for hf in range(2):
                pe.wait_ge(M["x1"], hf + 1)
                if hf == 1:
                    pe.wait_ge(M["params_sb"], 1)
                transposes((7, 0)[hf], XN[:, HT * hf:HT * hf + HT, :], F["x1T"])
            for hf in range(2):
                pe.wait_ge(M["x1T_sb"], hf + 1)
                pe.matmul(ps[:, 1 + hf, :], wkqv[:, 0, :], XT[:, hf, :], start=True, stop=True).then_inc(F["k"], 1)
                pe.wait_ge(M["vm_sb"], 1 + hf)
                pe.matmul(ps[:, 3 + hf, :], wkqv[:, 1, :], XT[:, hf, :], start=True, stop=True).then_inc(F["q"], 1)

            pe.wait_ge(ld["q"], 64)
            pe.wait_ge(M["vm_sb"], 4)
            for n in range(6):
                last = pe.transpose(ps[0:32, 5 + n // 4, 128 * (n % 4):128 * (n % 4) + 128], lb_sb[:, n, :], ident[:])
            last.then_inc(F["lbT"], 1)
            pe.wait_ge(M["lbT_sb"], 1)
            pe.wait_ge(M["wdq_sb"], 1)
            for n in range(6):
                o = ps[:, 5 + n // 4, 128 * (n % 4):128 * (n % 4) + 128]
                pe.matmul(o, wdq[:, n, :], ident[:], start=True, stop=False)
                last = pe.matmul(o, la_sb[:, n, :], lbT[:, n, :], start=False, stop=True)
            last.then_inc(F["weT"], 1)
            pe.wait_ge(ld["l1"], 64)
            for hf in range(2):
                pe.wait_ge(M["x1T_sb"], hf + 1)
                tokens_out((7, 0)[hf], CT[:, hf, :], wqkv1[:, 1, :]).then_inc(F["k1"], 1)
                pe.wait_ge(M["k_sb"], hf + 1)
                tokens_out(1 + hf, CT[:, hf, :], wqkv1[:, 2, :]).then_inc(F["v1"], 1)
            kv_bank = (3, 4, 5, 6, 7, 0)
            for g in range(6):
                if g == 0:
                    pe.wait_ge(M["q_sb"], 2)
                    pe.wait_ge(M["weT_sb"], 1)
                    pe.wait_ge(M["k1_read"], 2)
                    pe.wait_ge(M["kp_sb"], 2)
                    pe.wait_ge(M["vx_sb"], 2)
                for k, b in enumerate(kv_batches(g)):
                    h0 = 64 * (b % 2)
                    last = pe.matmul(ps[:, kv_bank[g], 132 * k:132 * k + 130], kp[h0:h0 + 64, b // 2, :],
                                     vx[h0:h0 + 64, b // 2, 0:130], start=True, stop=True)
                last.then_inc(F["kv"], 1)

            def scores(c):
                if c == 0:
                    pe.wait_ge(M["kvx_sb"], 6)
                    pe.wait_ge(M["v1_read"], 2)
                    pe.wait_ge(M["q_sb"], 2)
                if c == 0 or c == 2:
                    pe.wait_ge(ld["kmask"], 256 * 2)
                if c > 0:
                    pe.wait_ge(M["centered"], c)
                for tp in range(2):
                    for hb in range(2):
                        bank = 2 * tp + hb
                        pe.matmul(ps[:, bank, :], identb[:], causal[:].rearrange("p a s -> p (a s)"), start=True, stop=False)
                        for b in range(2):
                            tok = (2 * c + tp) * 128 + 64 * b
                            last = pe.matmul(ps[64 * b:64 * b + 64, bank, :], qT[:, tok // HALF, tok % HALF:tok % HALF + S],
                                             Km[:, 8 * hb:8 * hb + 8, tok:tok + S], start=False, stop=True)
                last.then_inc(F["scores"], 1)

            scores(0)
            for c in range(4):
                if c < 3:
                    scores(c + 1)
                pe.wait_ge(M["exped"], c + 1)
                for gq in range(4):
                    n = 4 * c + gq
                    if n >= 2:
                        pe.wait_ge(M["probsT_sb"], n - 1)
                    tp = gq // 2
                    for k in range(4):
                        pr = 4 * (gq % 2) + k
                        last = pe.transpose(ps[:, 4 + n % 2, 128 * k:128 * k + 128],
                                            P[:, tp, 2 * pr:2 * pr + 2, :].rearrange("p a s -> p (a s)"), ident[:])
                    last.then_inc(F["probsT"], 1)
                pe.wait_ge(M["sums"], c + 1)
                if c > 0:
                    pe.wait_ge(M["heads_sb"], c)
                for tp in range(2):
                    last = pe.transpose(ps[0:NH, 7, 128 * tp:128 * tp + 128], rc[:, tp, :], ident[:])
                last.then_inc(F["recT"], 1)
                pe.wait_ge(M["recT_sb"], c + 1)
                pe.matmul(ps[:, 7, 256:512], hmT[:], rT[:], start=True, stop=True).then_inc(F["rec"], 1)
                pe.wait_ge(M["probsT_sb"], 4 * c + 4)
                for b in range(4):
                    for r in range(4):
                        last = pe.matmul(ps[32 * r:32 * r + 32, 6, 128 * b:128 * b + 128],
                                         Vm[:, 4 * c + b, 32 * r:32 * r + 32],
                                         PT[:, b // 2, 2 * r:2 * r + 2, 64 * (b % 2):64 * (b % 2) + 64],
                                         start=True, stop=True)
                last.then_inc(F["heads"], 1)

            pe.wait_ge(ld["mlp"], 32)
            for hf in range(2):
                pe.wait_ge(M["AT_sb"], 2 * hf + 2)
                if hf == 1:
                    pe.wait_ge(M["heads_sb"], 4)
                    pe.wait_ge(M["probsT_sb"], 16)
                else:
                    pe.wait_ge(M["centered"], 4)
                for j in range(4):
                    if hf == 1:
                        pe.wait_ge(M["up_sb"], 4)
                    pe.matmul(ps[:, 4 * hf + j, :], w1_sb[:, j, :], AT[:, hf, :], start=True, stop=True).then_inc(F["up"], 1)
                pe.wait_ge(M["up_sb"], 4 * hf + 4)
                pe.wait_ge(ld["rows"], 16 * 8)
                for t in range(HT):
                    o = ps[:, hf, 128 * t:128 * t + 128]
                    for j in range(4):
                        pe.matmul(o, H1[:, j, 128 * t:128 * t + 128], w2_sb[:, j, :], start=(j == 0), stop=False)
                    last = pe.matmul(o, ones[:], rows[:, 0, :], start=False, stop=True)
                last.then_inc(F["down"], 1)

            for hf in range(2):
                pe.wait_ge(M["x2"], hf + 1)
                transposes(2 + hf, XN[:, HT * hf:HT * hf + HT, :], F["x2T"])
            for i in range(3):
                for hf in range(2):
                    if i == 0:
                        pe.wait_ge(M["x2T_sb"], hf + 1)
                        pe.wait_ge(M["up_sb"], 8)
                    else:
                        pe.wait_ge(M["z_sb"], 2 * (i - 1) + hf + 1)
                    tokens_out(4 + hf, hT[:, hf, :], weT[:, 2 * i, :], rows[:, 1 + i, :]).then_inc(F["y"], 1)
                for hf in range(2):
                    pe.wait_ge(M["yn"], 2 * i + hf + 1)
                    transposes(6 + hf, YN[:, HT * hf:HT * hf + HT, :], F["yT"])
                for hf in range(2):
                    pe.wait_ge(M["gT_sb"], 2 * i + hf + 1)
                    if i < 2:
                        if i == 0:
                            pe.wait_ge(M["X1"], hf + 1)
                        pe.matmul(ps[:, hf, :], weT[:, 2 * i + 1, :], gT[:, hf, :], start=True, stop=True).then_inc(F["z"], 1)
                    else:
                        tokens_out(hf, gT[:, hf, :], weT[:, 5, :], rows[:, 4, :],
                                   extra=[(hT[:, hf, :], ident[:])]).then_inc(F["z"], 1)

            for hf in range(2):
                pe.wait_ge(M["x3"], hf + 1)
                transposes(2 + hf, XN[:, HT * hf:HT * hf + HT, :], F["x3T"])
            for hf in range(2):
                pe.wait_ge(M["x3T_sb"], hf + 1)
                tokens_out(4 + hf, XT[:, hf, :], wqkv1[:, 0, :]).then_inc(F["q1"], 1)
            for hf in range(2):
                pe.wait_ge(M["q1_read"], hf + 1)
                transposes(6 + hf, YN[:, HT * hf:HT * hf + HT, :], F["q1T"])
            for hf in range(2):
                pe.wait_ge(M["q1T_sb"], hf + 1)
                pe.wait_ge(M["X2"], 2)
                for t in range(HT):
                    for b in range(2):
                        last = pe.matmul(ps[64 * b:64 * b + 64, 2 * hf + t // 2, 144 * (t % 2):144 * (t % 2) + 144],
                                         qT[:, hf, 128 * t + 64 * b:128 * t + 64 * b + 64],
                                         kvx[:, 8 * hf + 2 * t + b, :], start=True, stop=True)
                last.then_inc(F["att"], 1)
            for hf in range(2):
                pe.wait_ge(M["att_sb"], hf + 1)
                for e in range(HD):
                    last = pe.transpose(ps[0:64, 4 + 2 * hf + e // 4, 128 * (e % 4):128 * (e % 4) + 128],
                                        AO[:, HT * hf:HT * hf + HT, e:D:HD], ident[:])
                last.then_inc(F["hE"], 1)
            for hf in range(2):
                pe.wait_ge(M["hE_sb"], 2 * hf + 2)
                for m in range(8):
                    last = pe.transpose(ps[:, 2 * hf, 64 * m:64 * m + 64], hE[:, hf, 16 * m:16 * m + 16, :], ident[0:64, 0:64])
                last.then_inc(F["attT"], 1)
            for hf in range(2):
                pe.wait_ge(M["attT_sb"], hf + 1)
                tokens_out(4 + hf, AT[:, hf, :], dw_sb[:], rows[:, 5, :]).then_inc(F["dense"], 1)
            for hf in range(2):
                pe.wait_ge(M["x4"], hf + 1)
                transposes(hf, XN[:, HT * hf:HT * hf + HT, :], F["x4T"])
            for hf in range(2):
                pe.wait_ge(M["x4T_sb"], hf + 1)
                for t in range(HT):
                    last = pe.matmul(ps[:, 2 + hf, 8 * t:8 * t + 8], XT[:, hf, 128 * t:128 * t + 128],
                                     PC[:, R_GATE:R_GATE + 8], start=True, stop=True)
                last.then_inc(F["gate"], 1)

            pe.wait_ge(M["gate_read"], 2)
            with pe.Fori(0, E // 2) as i:
                for slot in range(2):
                    pe.wait_ge(ld_e[slot], 48 * (i + 1))
                    for hf in range(2):
                        for j, (k0, kn_) in enumerate(KC):
                            pe.wait_ge(M["act_sb"], 12 * i + 6 * slot + 3 * hf + j + 1)
                            for u in range(2):
                                mm = pe.matmul(ps[0:kn_, 2 * j + u, :], ew1[:, slot, u * INTER + k0:u * INTER + k0 + kn_],
                                               XT[:, hf, :], start=True, stop=True)
                            mm.then_inc(F["h%d" % j], 1)
                        pe.wait_ge(M["act_sb"], 12 * i + 6 * slot + 3 * hf + 6)
                        pe.wait_ge(M["oe_read"], 4 * i + 2 * slot + hf + 1)
                        for t in range(HT):
                            for j, (k0, kn_) in enumerate(KC):
                                last = pe.matmul(ps[:, 6 + hf, 128 * t:128 * t + 128], am[0:kn_, j, 128 * t:128 * t + 128],
                                                 ew2[0:kn_, slot, j, :], start=(j == 0), stop=(j == 2))
                        last.then_inc(F["oe"], 1)

        @block.scalar
        def _(act):
            a = nc.scalar
            act.wait_ge(ld["gates"], 32)
            a.activation(tg[:], gts[:], ACT.Tanh).then_inc(M["tanh_sb"], 1)
            for hf in range(2):
                act.wait_ge(F["ctxT"], hf + 1)
                a.copy(CT[:, hf, :], ps[:, 1 + hf, :]).then_inc(M["ctxT_sb"], 1)
            for hf in range(2):
                act.wait_ge(F["x1T"], hf + 1)
                a.copy(XT[:, hf, :], ps[:, (7, 0)[hf], :]).then_inc(M["x1T_sb"], 1)
            act.wait_ge(M["params_sb"], 1)
            for hf in range(2):
                act.wait_ge(F["k"], hf + 1)
                a.activation(kT[:, hf, :], ps[:, 1 + hf, :], ACT.Identity, bias=PC[:, R_BK:R_BK + 1]).then_inc(M["k_sb"], 1)
                act.wait_ge(F["q"], hf + 1)
                a.activation(qT[:, hf, :], ps[:, 3 + hf, :], ACT.Identity, bias=PC[:, R_BQ:R_BQ + 1]).then_inc(M["q_sb"], 1)
            act.wait_ge(F["lbT"], 1)
            a.copy(lbT[:, 0:4, :].rearrange("p n d -> p (n d)"), ps[0:32, 5, :])
            a.copy(lbT[:, 4:6, :].rearrange("p n d -> p (n d)"), ps[0:32, 6, 0:256]).then_inc(M["lbT_sb"], 1)
            act.wait_ge(F["weT"], 1)
            a.copy(weT[:, 0:4, :].rearrange("p n d -> p (n d)"), ps[:, 5, :])
            a.copy(weT[:, 4:6, :].rearrange("p n d -> p (n d)"), ps[:, 6, 0:256]).then_inc(M["weT_sb"], 1)
            for c in range(4):
                act.wait_ge(M["centered"], c + 1)
                a.activation(P[:], P[:], ACT.Exp).then_inc(M["exped"], 1)
                for gq in range(4):
                    n = 4 * c + gq
                    act.wait_ge(F["probsT"], n + 1)
                    if c > 0:
                        act.wait_ge(F["heads"], c)
                    a.copy(PT[:, gq // 2, 4 * (gq % 2):4 * (gq % 2) + 4, :].rearrange("p n q -> p (n q)"),
                           ps[:, 4 + n % 2, :]).then_inc(M["probsT_sb"], 1)
                act.wait_ge(M["heads_sb"], c + 1)
                a.activation(AT[:, c // 2, 256 * (c % 2):256 * (c % 2) + 256], o2[:].rearrange("p b s -> p (b s)"),
                             ACT.Identity, bias=PC[:, R_BV:R_BV + 1]).then_inc(M["AT_sb"], 1)
            for hf in range(2):
                if hf == 1:
                    act.wait_ge(F["down"], 1)
                for j in range(4):
                    act.wait_ge(F["up"], 4 * hf + j + 1)
                    a.activation(H1[:, j, :], ps[:, 4 * hf + j, :], ACT.Gelu,
                                 bias=PC[:, R_B1 + j:R_B1 + j + 1]).then_inc(M["up_sb"], 1)
            for hf in range(2):
                act.wait_ge(F["x2T"], hf + 1)
                a.copy(hT[:, hf, :], ps[:, 2 + hf, :]).then_inc(M["x2T_sb"], 1)
            for i in range(3):
                for hf in range(2):
                    act.wait_ge(F["yT"], 2 * i + hf + 1)
                    a.activation(gT[:, hf, :], ps[:, 6 + hf, :], ACT.Gelu, bias=PC[:, R_FBETA + i:R_FBETA + i + 1],
                                 scale=PC[:, R_FG + i:R_FG + i + 1]).then_inc(M["gT_sb"], 1)
            for hf in range(2):
                act.wait_ge(F["x3T"], hf + 1)
                a.copy(XT[:, hf, :], ps[:, 2 + hf, :]).then_inc(M["x3T_sb"], 1)
            for hf in range(2):
                act.wait_ge(F["q1T"], hf + 1)
                a.activation(kT[:, hf, :], ps[:, 6 + hf, :], ACT.Relu, bias=PC[:, R_LB:R_LB + 1],
                             scale=PC[:, R_LG:R_LG + 1]).then_inc(M["relu_sb"], 1)
            for hf in range(2):
                act.wait_ge(F["hE"], hf + 1)
                for u in range(2):
                    a.copy(hE[:, hf, :, 4 * u:4 * u + 4].rearrange("p n e -> p e n"),
                           ps[0:64, 4 + 2 * hf + u, :].rearrange("p (e n) -> p e n", e=4)).then_inc(M["hE_sb"], 1)
            for hf in range(2):
                act.wait_ge(F["attT"], hf + 1)
                for b in range(2):
                    last = a.copy(AT[:, hf, :].rearrange("c (t b h q) -> c b q t h", t=HT, b=2, h=NH)[:, b],
                                  ps[:, 2 * hf, 256 * b:256 * b + 256].rearrange("c (q t h) -> c q t h", q=4, t=HT))
                last.then_inc(M["attT_sb"], 1)
            for hf in range(2):
                act.wait_ge(F["x4T"], hf + 1)
                a.copy(XT[:, hf, :], ps[:, hf, :]).then_inc(M["x4T_sb"], 1)
            act.wait_ge(M["dlog"], 1)
            a.activation(el[:], dl[:], ACT.Exp).then_inc(M["el_sb"], 1)
            with act.Fori(0, E // 2) as i:
                for k in range(4):
                    for j, (k0, kn_) in enumerate(KC):
                        act.wait_ge(F["h%d" % j], 4 * i + k + 1)
                        act.wait_ge(M["act_sb"], 12 * i + 3 * k + j + 1)
                        a.activation(sg[0:kn_, j, :], ps[0:kn_, 2 * j, :], ACT.Silu).then_inc(M["silu"], 1)

        @block.vector
        def _(dve):
            v = nc.vector
            n = [0]

            def link(ins):
                n[0] += 1
                ins.then_inc(dve_step, 1)
                dve.wait_ge(dve_step, n[0])

            k = [0]

            def stats(src):
                for t in range(HT):
                    ins = v.bn_stats(bst[:, t, :], src[:, t, :])
                link(ins)
                for t in range(HT):
                    ins = v.bn_aggr(mv[:, k[0], t, :], bst[:, t, :])
                ins.then_inc(M["ln_var"], 1)
                k[0] += 1
                dve.wait_ge(M["ln_var"], k[0])
                return k[0] - 1

            def normalize(i, src, dst):
                dve.wait_ge(M["ln_rstd"], i + 1)
                for t in range(HT):
                    ins = v.tensor_scalar(dst[:, t, :], src[:, t, :], mv[:, i, t, 0:1], rstd[:, i, t:t + 1],
                                          ALU.subtract, ALU.mult)
                return ins

            def tiles(t, hf):
                return t[:, HT * hf:HT * hf + HT, :]

            def bank(b):
                return ps[:, b, :].rearrange("p (t d) -> p t d", t=HT)

            dve.wait_ge(ld["x"], 16)
            ids = [stats(tiles(X, hf)) for hf in range(2)]
            for hf in range(2):
                normalize(ids[hf], tiles(X, hf), tiles(XN, hf)).then_inc(M["x1"], 1)
            dve.wait_ge(F["params"], 1)
            v.tensor_copy(PC[:], ps[:, 0, 0:R_END]).then_inc(M["params_sb"], 1)
            dve.wait_ge(consts, 1)
            for c in range(4):
                dve.wait_ge(F["v"], c + 1)
                v.tensor_tensor(Vm[:, 4 * c:4 * c + 4, :], ps[:, 3 + c, :].rearrange("p (b d) -> p b d", b=4),
                                par[:].rearrange("p h d -> p (h d)").unsqueeze(1).to_broadcast([128, 4, 128]),
                                ALU.mult).then_inc(M["vm_sb"], 1)
            dve.wait_ge(ld["q"], 64)
            link(v.tensor_copy(wf, qw_sb[:]))
            link(v.tensor_scalar(wf, wf, 1.0 / 7.5, -1.0, ALU.mult, ALU.add))
            v.tensor_tensor(wdq[:].rearrange("p n (g k) -> p (n g) k", g=8),
                            wf.rearrange("p n (g k) -> p (n g) k", g=8),
                            sc_sb[:].rearrange("p n g -> p (n g)").unsqueeze(2).to_broadcast([128, 48, 16]),
                            ALU.mult).then_inc(M["wdq_sb"], 1)
            v.tensor_copy(blk[:], hm[:].unsqueeze(2).to_broadcast([128, NH, HD]))
            v.tensor_reduce(pairsel[:, 0:2], hm[:].rearrange("p (r s j) -> p s r j", r=4, s=2), axis=AX.XY, op=ALU.add)
            dve.wait_ge(ld["rows"], 16 * 8)
            for hf in range(2):
                for src, bk_, read in ((kn, (7, 0)[hf], "k1"), (vn, 1 + hf, "v1")):
                    dve.wait_ge(F[read], hf + 1)
                    i = stats(bank(bk_))
                    normalize(i, bank(bk_), tiles(src, hf)).then_inc(M[read + "_read"], 1)
                    dve.wait_ge(M[read + "_read"], hf + 1)
                    link(v.tensor_tensor(tiles(src, hf), tiles(src, hf), bcast[:, 0, :].unsqueeze(1).to_broadcast([128, HT, D]), ALU.mult))
                    link(v.tensor_tensor(tiles(src, hf), tiles(src, hf), bcast[:, 1, :].unsqueeze(1).to_broadcast([128, HT, D]), ALU.add))
                    if src is kn:
                        link(v.tensor_scalar(tiles(src, hf), tiles(src, hf), 0.0, 1e-6, ALU.max, ALU.add))
                    for t in range(HT):
                        g = HT * hf + t
                        ins = v.tensor_scalar(kp[:, g, :] if src is kn else vx[:, g, 0:D], src[:, g, :],
                                              PC[:, R_MASK + g:R_MASK + g + 1], None, ALU.mult)
                    ins.then_inc(M["kp_sb" if src is kn else "vx_sb"], 1)
            for g in range(6):
                dve.wait_ge(F["kv"], g + 1)
                bs = kv_batches(g)
                nb = len(bs)
                kvb = ps[:, (3, 4, 5, 6, 7, 0)[g], 0:132 * nb].rearrange("p (b d) -> p b d", b=nb)
                v.tensor_tensor(kvx[:, bs[0]:bs[-1] + 1:2, 0:D], kvb[:, :, 0:D],
                                blk[:].rearrange("p h d -> p (h d)").unsqueeze(1).to_broadcast([128, nb, D]), ALU.mult)
                for b in range(nb):
                    ins = v.tensor_scalar(kvx[:, bs[b], D:D + NH], hm[:], kvb[:, b, D:D + 1], None, ALU.mult)
                ins.then_inc(M["kvx_sb"], 1)

            for c in range(4):
                sc = ps[:, 0:4, :].rearrange("p (t u) (h s) -> p (t u h) s", t=2, s=S)
                dve.wait_ge(F["scores"], c + 1)
                link(v.tensor_reduce(mx[:].rearrange("p t h -> p (t h)"), sc, axis=AX.X, op=ALU.max))
                if c > 0:
                    dve.wait_ge(F["probsT"], 4 * c)
                    dve.wait_ge(M["sums"], c)
                Pv = P[:].rearrange("p t h s -> p (t h) s")
                v.tensor_tensor(Pv, sc, mx[:].rearrange("p t h -> p (t h)").unsqueeze(2).to_broadcast([128, 32, S]),
                                ALU.subtract).then_inc(M["centered"], 1)
                dve.wait_ge(M["exped"], c + 1)
                link(v.tensor_reduce(sm[:].rearrange("p t h -> p (t h)"), Pv, axis=AX.X, op=ALU.add))
                v.reciprocal(rc[:], sm[:]).then_inc(M["sums"], 1)
                dve.wait_ge(F["recT"], c + 1)
                v.tensor_copy(rT[:], ps[0:NH, 7, 0:256]).then_inc(M["recT_sb"], 1)
                dve.wait_ge(F["heads"], c + 1)
                dve.wait_ge(F["rec"], c + 1)
                if c > 0:
                    dve.wait_ge(M["AT_sb"], c)
                ob = ps[:, 6, :].rearrange("p (b j q) -> p b j q", b=4, j=2)
                link(v.tensor_scalar(o0[:], ob[:, :, 0, :], pairsel[:, 0:1], None, ALU.mult))
                link(v.scalar_tensor_tensor(o1[:], ob[:, :, 1, :], pairsel[:, 1:2], o0[:], ALU.mult, ALU.add))
                v.tensor_tensor(o2[:].rearrange("p b s -> p (b s)"), o1[:].rearrange("p b s -> p (b s)"),
                                ps[:, 7, 256:512], ALU.mult).then_inc(M["heads_sb"], 1)

            def add_gated(g, b, hf, signal):
                v.scalar_tensor_tensor(tiles(X, hf).rearrange("p t d -> p (t d)"), ps[:, b, :], tg[:, g:g + 1],
                                       tiles(X, hf).rearrange("p t d -> p (t d)"), ALU.mult, ALU.add).then_inc(M[signal], 1)

            def norm_x(signal, x_signal):
                ids = []
                for hf in range(2):
                    dve.wait_ge(M[x_signal], hf + 1)
                    ids.append(stats(tiles(X, hf)))
                for hf in range(2):
                    normalize(ids[hf], tiles(X, hf), tiles(XN, hf)).then_inc(M[signal], 1)

            dve.wait_ge(M["tanh_sb"], 1)
            for hf in range(2):
                dve.wait_ge(F["down"], hf + 1)
                add_gated(0, hf, hf, "X1")
            norm_x("x2", "X1")
            for i in range(3):
                ids = []
                for hf in range(2):
                    dve.wait_ge(F["y"], 2 * i + hf + 1)
                    ids.append(stats(bank(4 + hf)))
                for hf in range(2):
                    normalize(ids[hf], bank(4 + hf), tiles(YN, hf)).then_inc(M["yn"], 1)
                for hf in range(2):
                    dve.wait_ge(F["z"], 2 * i + hf + 1)
                    if i < 2:
                        v.scalar_tensor_tensor(hT[:, hf, :], ps[:, hf, :], PC[:, R_FB + 2 * i + 1:R_FB + 2 * i + 2],
                                               hT[:, hf, :], ALU.add, ALU.add).then_inc(M["z_sb"], 1)
                    else:
                        add_gated(2, hf, hf, "X2")
            norm_x("x3", "X2")
            ids = []
            for hf in range(2):
                dve.wait_ge(F["q1"], hf + 1)
                ids.append(stats(bank(4 + hf)))
            for hf in range(2):
                normalize(ids[hf], bank(4 + hf), tiles(YN, hf)).then_inc(M["q1_read"], 1)
            for hf in range(2):
                dve.wait_ge(M["relu_sb"], hf + 1)
                v.tensor_scalar(qT[:, hf, :], kT[:, hf, :], 1e-6, None, ALU.add).then_inc(M["q1T_sb"], 1)
            for hf in range(2):
                dve.wait_ge(F["att"], hf + 1)
                for u in range(2):
                    z = zz[:, 2 * hf + u]
                    av = ps[:, 2 * hf + u, 0:288].rearrange("p (t c) -> p t c", t=2)
                    link(v.tensor_scalar(z, av[:, :, D:D + NH], 1e-6, None, ALU.add))
                    link(v.reciprocal(z, z))
                    ins = v.tensor_tensor(AO[:, HT * hf + 2 * u:HT * hf + 2 * u + 2, :].rearrange("p t (h d) -> p t h d", h=NH),
                                          av[:, :, 0:D].rearrange("p t (h d) -> p t h d", h=NH),
                                          z.unsqueeze(3).to_broadcast([128, 2, NH, HD]), ALU.mult)
                ins.then_inc(M["att_sb"], 1)
            ids = []
            for hf in range(2):
                dve.wait_ge(F["dense"], hf + 1)
                ids.append(stats(bank(4 + hf)))
            for hf in range(2):
                ins = normalize(ids[hf], bank(4 + hf), tiles(YN, hf))
                ins.then_inc(M["dense_read"], 1)
                dve.wait_ge(M["dense_read"], hf + 1)
                y = tiles(YN, hf)
                link(v.tensor_tensor(y, y, bcast[:, 0, :].unsqueeze(1).to_broadcast([128, HT, D]), ALU.mult))
                link(v.tensor_tensor(y, y, bcast[:, 1, :].unsqueeze(1).to_broadcast([128, HT, D]), ALU.add))
                v.scalar_tensor_tensor(tiles(X, hf), y, tg[:, 1:2], tiles(X, hf), ALU.mult, ALU.add).then_inc(M["X3"], 1)
            norm_x("x4", "X3")

            for hf in range(2):
                dve.wait_ge(F["gate"], hf + 1)
                v.tensor_copy(lg[:, HT * hf:HT * hf + HT, :], ps[:, 2 + hf, 0:32].rearrange("p (t e) -> p t e", t=HT)).then_inc(M["gate_read"], 1)
            dve.wait_ge(M["gate_read"], 2)
            for t in range(T):
                ins = v.max(top[:, t, :], lg[:, t, :])
            link(ins)
            v.tensor_tensor(dl[:], top[:, :, 1], top[:, :, 0], ALU.subtract).then_inc(M["dlog"], 1)
            for t in range(T):
                ins = v.max_index(topi[:, t, :], top[:, t, :], lg[:, t, :])
            link(ins)
            link(v.tensor_copy(topf[:], topi[:]))
            dve.wait_ge(M["el_sb"], 1)
            link(v.tensor_scalar(den[:], el[:], 1.0, None, ALU.add))
            link(v.reciprocal(tw[:, :, 0], den[:]))
            link(v.tensor_tensor(tw[:, :, 1], tw[:, :, 0], el[:], ALU.mult))
            link(v.tensor_scalar(tw[:], tw[:], tg[:, 3:4], None, ALU.mult))
            for s in range(2):
                link(v.tensor_tensor(oh[:, s], iota8[:].unsqueeze(1).to_broadcast([128, T, 8]),
                                     topf[:, :, s:s + 1].to_broadcast([128, T, 8]), ALU.is_equal))
                link(v.tensor_tensor(oh[:, s], oh[:, s], tw[:, :, s:s + 1].to_broadcast([128, T, 8]), ALU.mult))
            v.tensor_tensor(wexp[:], oh[:, 0], oh[:, 1], ALU.add).then_inc(M["wexp_sb"], 1)
            dve.wait_ge(M["wexp_sb"], 1)
            v.engine_nop().then_inc(M["act_sb"], 3)
            v.engine_nop().then_inc(M["oe_read"], 2)
            with dve.Fori(0, E // 2) as i:
                for kk in range(4):
                    hf = kk % 2
                    slot = kk // 2
                    dve.wait_ge(F["oe"], 4 * i + kk)
                    v.tensor_copy(wcur[:, kk, :].unsqueeze(2), wexp[:, HT * hf:HT * hf + HT, bass.ds(2 * i + slot, 1)])
                    for j, (k0, kn_) in enumerate(KC):
                        dve.wait_ge(M["silu"], 12 * i + 3 * kk + j + 1)
                        v.tensor_tensor(am[0:kn_, j, :], ps[0:kn_, 2 * j + 1, :], sg[0:kn_, j, :], ALU.mult).then_inc(M["act_sb"], 1)
                    dve.wait_ge(F["oe"], 4 * i + kk + 1)
                    dve.wait_ge(M["oe_read"], 4 * i + kk + 2)
                    for t in range(HT):
                        g = HT * hf + t
                        ins = v.scalar_tensor_tensor(X[:, g, :], ps[:, 6 + hf, 128 * t:128 * t + 128],
                                                     wcur[:, kk, t:t + 1], X[:, g, :], ALU.mult, ALU.add)
                    ins.then_inc(M["oe_read"], 1)
            dve.wait_ge(M["oe_read"], 18)
            v.engine_nop().then_inc(M["X4"], 1)


LN_1E6 = (2, 3, 4, 5, 16, 17, 18, 19)

_INS = ['x', 'ctx_1024', 'mask_BxS2_ff1', 'g_xattn', 'g_ffn', 'L0_xattn_Wk', 'L0_xattn_bk', 'L0_xattn_Wq', 'L0_xattn_bq',
        'L0_xattn_Wv', 'L0_xattn_bv', 'L0_xattn_W1', 'L0_xattn_b1', 'L0_xattn_W2', 'L0_xattn_b2', 'L0_ffn_qweights',
        'L0_ffn_scales', 'L0_ffn_biases', 'L0_ffn_lora_a', 'L0_ffn_lora_b', 'L0_ffn_ln_gamma', 'L0_ffn_ln_beta',
        'L1_xattn_wq', 'L1_xattn_wk', 'L1_xattn_wv', 'L1_xattn_ln_gamma', 'L1_xattn_ln_beta', 'L1_xattn_dense_w',
        'L1_xattn_dense_b', 'L1_ffn_gate_w', 'L1_ffn_w1_stacked', 'L1_ffn_w2_stacked']


def kernel(**inputs):
    import numpy as _np
    import concourse.bacc as _bacc
    from concourse import mybir as _mybir
    from concourse.bass_utils import run_bass_kernel_spmd as _run

    nc = _bacc.Bacc("TRN2", target_bir_lowering=False, num_devices=1)
    arrays, args = {}, []
    for name in _INS:
        a = _np.ascontiguousarray(inputs[name])
        arrays[f"in_{name}_dram"] = a
        args.append(nc.dram_tensor(f"in_{name}_dram", a.shape, _mybir.dt.from_np(a.dtype), kind="ExternalInput").ap())
    out = nc.dram_tensor("out_0_dram", (16, 64, 128), _mybir.dt.float32, kind="ExternalOutput").ap()
    flamingo(nc, *args, out)
    r = _run(nc, [arrays], core_ids=[0])
    return r.results[0]["out_0_dram"]
```

```python
from contextlib import ExitStack

import concourse.bass as bass
from concourse import mybir

ALU = mybir.AluOpType
ACT = mybir.ActivationFunctionType
AX = mybir.AxisListType
F32 = mybir.dt.float32
BF16 = mybir.dt.bfloat16
I32 = mybir.dt.int32
U32 = mybir.dt.uint32

D = 128
S = 64
T = 8
HT = 4
HALF = 512
NH = 16
HD = 8
E = 8
INTER = 352
KC = [(0, 128), (128, 128), (256, 96)]
NEG = -1.0e30

R_BK, R_BQ, R_BV, R_B1, R_FB, R_FG, R_FBETA, R_LG, R_LB, R_GATE, R_MASK, R_END = 0, 1, 2, 3, 7, 13, 16, 19, 20, 21, 29, 37


def kv_batches(hf, g):
    return [8 * hf + 2 * m + g % 2 for m in (range(3), [3])[g // 2]]


def down_chain(hf):
    ffn = [(n, hf, i) for i in range(3) for n in ("y", "yT", "z")]
    return [(n, hf) for n in ("up", "down", "x2T")] + ffn + [
        (n, hf) for n in ("x3T", "q1", "q1T", "att", "hE", "attT", "dense", "X3", "x4T", "gate", "route")]


ORDER = """
    x1.0 ctxT.0 ctxT.1 x1.1 params kq.0 K.0 v.0 KP.0 v.1 v.2 KP.1 v.3 weights S.0 rows K.1 kq.1 M.0 lbT k1.0 KP.2
    S.1 K.2 k1n.0 M.1 v1.0 T1.0 S.2 KP.3 v1n.0 T1.1 k1.1 T2.0 M.2 k1n.1 k1a.0 weT K.3 T3.0 v1.1 S.3 T2.1 T1.2 T3.1
    T2.2 M.3 T3.2 T1.3 T2.3 k1a.1 T3.3 KP.4 up.0 v1n.1 K.4 v1a.0 kv.0.0 K.5 down.0 KP.5 S.4 x2T.0 K.6 y.0.0 yT.0.0
    M.4 z.0.0 T1.4 y.0.1 T2.4 S.5 yT.0.1 v1a.1 KP.6 M.5 K.7 KP.7 kv.0.1 T3.4 z.0.1 T1.5 y.0.2 kv.0.2 S.6 T2.5
    yT.0.2 M.6 T3.5 kv.0.3 z.0.2 S.7 T1.6 x3T.0 M.7 beta.0 T2.6 kv.1.0 T3.6 T1.7 q1.0 T2.7 T3.7 up.1 q1T.0 q1e.0
    down.1 att.0 hE.0 x2T.1 attT.0 y.1.0 yT.1.0 dense.0 kv.1.1 z.1.0 X3.0 y.1.1 x4T.0 gate.0 yT.1.1 route.0 kv.1.2
    z.1.1 kv.1.3 y.1.2 yT.1.2 C.0 z.1.2 G.0 C.1 x3T.1 q1.1 q1T.1 q1e.1 beta.1 att.1 C.2 G.1 hE.1 C.3 attT.1 G.2
    dense.1 X3.1 G.3 C.4 P.0.0 P.0.1 C.5 G.4 x4T.1 C.6 A.0 G.5 gate.1 C.7 P.1.0 G.6 G.7 route.1 C.8 G.8 P.1.1 C.9
    A.1 C.10 G.9 C.11 P.2.0 P.2.1 G.10 G.11 A.2 C.12 C.13 G.12 P.3.0 G.13 C.14 G.14 P.3.1 C.15 A.3 P.4.0 G.15 P.4.1
    C.16 A.4 G.16 C.17 C.18 G.17 C.19 P.5.0 G.18 C.20 G.19 P.5.1 G.20 A.5 C.21 C.22 G.21 C.23 G.22 P.6.0 P.6.1 G.23
    A.6 rounds
"""
ORDER = [tuple(int(w) if w.isdigit() else w for w in step.split(".")) for step in ORDER.split()]


def nth(name, hf, i):
    return [s for s in ORDER if s[0] == name].index((name, hf, i))


PAIR = ((0, 1), (5, 6))
LN_STEPS = [s for s in ORDER if s[0] in ("x1", "k1", "v1", "down", "y", "q1", "dense", "X3") or (s[0] == "z" and s[2] == 2)]
LN_SMALL = [s[0] in ("k1", "v1", "q1", "dense") for s in LN_STEPS]


def flamingo(nc, x, ctx_in, mask, g_xattn, g_ffn, Wk, bk, Wq, bq, Wv, bv, W1, b1, W2, b2,
             qw, scales, fbias, lora_a, lora_b, ln_g, ln_b, wq1, wk1, wv1, lg1, lb1,
             dense_w, dense_b, gate_w, w1s, w2s, out):
    with ExitStack() as ctx:
        def sb(name, shape, dt=F32):
            return ctx.enter_context(nc.sbuf_tensor(name, shape, dt))

        def sem(name):
            return ctx.enter_context(nc.semaphore(name))

        ps = ctx.enter_context(nc.psum_tensor("ps", [128, 8, 512], F32))

        X = sb("X", [128, T, D])
        CX = sb("CX", [128, T, D])
        PR = sb("PR", [R_END, 128])
        PC = sb("PC", [128, R_END])
        wkqv = sb("wkqv", [128, 3, D])
        w1_sb = sb("w1_sb", [128, 4, D])
        w2_sb = sb("w2_sb", [128, 4, D])
        rows = sb("rows", [6, D])
        rows_p = sb("rows_p", [6, 3, D], BF16)
        rows_r = sb("rows_r", [6, 2, D])
        rows_b = sb("rows_b", [3, 6, D], BF16)
        bcast = sb("bcast", [128, 2, D])
        gated_gb = sb("gated_gb", [128, 2, D])
        gts = sb("gts", [128, 4])
        tg = sb("tg", [128, 4])
        qw_sb = sb("qw_sb", [128, 6, D], I32)
        sc_sb = sb("sc_sb", [128, 6, 8])
        la_sb = sb("la_sb", [32, 6, D])
        lb_sb = sb("lb_sb", [128, 6, 32])
        wqkv1 = sb("wqkv1", [128, 3, D])
        dw_sb = sb("dw_sb", [128, D])
        ew1 = sb("ew1", [128, 2, 2 * INTER])
        ew2 = sb("ew2", [128, 2, 3, D])

        ident = sb("ident", [128, 128])
        identb = sb("identb", [128, 128], BF16)
        causal = sb("causal", [128, 8, S], BF16)
        hm = sb("hm", [128, NH])
        hmT = sb("hmT", [NH, 128])
        blk = sb("blk", [128, NH, HD])
        par = sb("par", [128, NH, HD])
        pairsel = sb("pairsel", [128, 4])
        neghalf = sb("neghalf", [128, HT])
        ones = sb("ones", [3, 128], BF16)
        iota8 = sb("iota8", [128, 8])

        XN = sb("XN", [128, T, D])
        XT = sb("XT", [128, 2, HALF])
        CT = sb("CT", [128, 2, HALF])
        kT = sb("kT", [128, 2, HALF])
        qT = sb("qT", [128, 2, HALF])
        Km = sb("Km", [128, 2, NH, 128])
        Vm = sb("Vm", [128, 16, D])
        P = sb("P", [128, 2, NH, S])
        PT = sb("PT", [128, 2, 8, 128])
        mx = sb("mx", [128, 2, NH])
        sm = sb("sm", [128, 2, NH])
        rc = sb("rc", [128, 2, NH])
        rT = sb("rT", [NH, 2, 128])
        o0 = sb("o0", [128, 2, 2, S])
        o1 = sb("o1", [128, 2, 2, S])
        o2 = sb("o2", [128, 2, 2, S])
        AT = sb("AT", [128, 2, HALF])
        hE = P[0:64].rearrange("p a h s -> p (a h s)").rearrange("p (f n e) -> p f n e", f=2, e=HD)
        H1 = sb("H1", [128, 4, HALF])
        wdq = sb("wdq", [128, 6, D])
        wf = H1[:].rearrange("p c (a d) -> p (c a) d", d=D)[:, 0:6, :]
        lbT = sb("lbT", [32, 6, D])
        weT = sb("weT", [128, 6, D])
        hT = sb("hT", [128, 2, HALF])
        YN = sb("YN", [128, T, D])
        gT = AT
        XB = sb("XB", [128, T, D])
        kp = sb("kp", [128, T, D])
        vx = sb("vx", [128, T, 132])
        kvx = sb("kvx", [128, 16, 144])
        zz = sb("zz", [128, 4, 2, NH])
        AO = CX
        kn = sb("kn", [128, T, D])
        vn = sb("vn", [128, T, D])
        bst = sb("bst", [128, HT, 6])
        NLN = len(LN_SMALL)
        mv = sb("mv", [128, NLN, HT, 2])
        ve = sb("ve", [128, NLN, HT])
        rstd = sb("rstd", [128, NLN, HT])
        lg = sb("lg", [128, T, 8])
        top = sb("top", [128, T, 8])
        topi = sb("topi", [128, T, 8], U32)
        topf = sb("topf", [128, T, 8])
        dl = sb("dl", [128, T])
        el = sb("el", [128, T])
        den = sb("den", [128, T])
        tw = sb("tw", [128, T, 2])
        oh = sb("oh", [128, T, 2, 8])
        wexp = sb("wexp", [128, T, 8])
        wcur = sb("wcur", [128, 2, HT])
        sg = sb("sg", [128, 2, HALF])
        am = sb("am", [128, 2, 3, HALF])

        names = ["bcast", "rows_b", "ctx", "pr", "wkqv", "mlp", "rows", "gates", "q", "l1"]
        ld = {n: sem("ld_" + n) for n in names}
        ld_x = [sem("ld_x_0"), sem("ld_x_1")]
        ld_w1 = [sem("ld_expert_w1_even"), sem("ld_expert_w1_odd")]
        ld_w2 = [sem("ld_expert_w2_even"), sem("ld_expert_w2_odd")]
        stored = sem("stored")
        consts = sem("consts_ready")
        hm_ready = sem("head_mask_ready")
        pool_step = sem("pool_step")
        dve_step = sem("dve_step")
        F = {n: sem("pe_" + n) for n in [
            "params", "ctxT", "v", "x1T", "k", "q", "lbT", "weT", "k1", "v1", "kv", "scores", "probsT", "heads",
            "recT", "up", "down", "x2T", "y", "yT", "z", "x3T", "q1", "q1T", "att", "hE", "attT", "dense",
            "x4T", "gate", "h", "oe"]}
        M = {n: sem(n) for n in [
            "params_sb", "ctxT_sb", "vm_sb", "x1", "x1T_sb", "k_sb", "q_sb", "wdq_sb", "lbT_sb", "weT_sb",
            "kp_sb", "vx_sb", "kvx_sb", "centered", "exped", "sums", "probsT_sb", "recT_sb",
            "heads_sb", "AT_sb", "up_sb", "x2", "x2T_sb", "yn", "gT_sb", "z_sb", "x3",
            "x3T_sb", "q1_read", "q1T_sb", "relu_sb", "att_sb", "hE_sb", "attT_sb", "dense_read", "x4", "x4T_sb",
            "gate_read", "dlog", "el_sb", "silu", "act_sb", "oe_read", "tanh_sb",
            "ln_var", "ln_rstd", "keys_lo", "keys_hi", "kn", "vn", "rows_split", "xb"]}

        block = ctx.enter_context(nc.Block())

        def dbank(hf, k):
            return ((5, 6), (2, 3))[hf][k]

        def place_keys(eng, calls, t, part):
            hf, hs = t // HT, slice(8 * part, 8 * part + 8)
            eng.wait_ge(M["k_sb"], hf + 1)
            if t > 1:
                eng.wait_ge(F["scores"], t - 1)
            calls.tensor_tensor(Km[:, t % 2, hs, :],
                                kT[:, hf, 128 * (t % HT):128 * (t % HT) + 128].unsqueeze(1).to_broadcast([128, 8, 128]),
                                hm[:, hs].unsqueeze(2).to_broadcast([128, 8, 128]),
                                ALU.mult).then_inc(M[("keys_lo", "keys_hi")[part]], 1)

        @block.sync
        def _(sp):
            xv = x.rearrange("(t b) s d -> (b s) t d", b=2)
            row = lambda a: a.rearrange("(a d) -> a d", d=128)
            for hf in range(2):
                sp.dma_start(X[:, HT * hf:HT * hf + HT, :], xv[:, HT * hf:HT * hf + HT, :]).then_inc(ld_x[hf], 16)
            for i, w in enumerate((Wk, Wq, Wv)):
                sp.dma_start(wkqv[:, i, :], w).then_inc(ld["wkqv"], 16)
            stack = [(R_BK, 1, row(bk)), (R_BQ, 1, row(bq)), (R_BV, 1, row(bv)), (R_B1, 4, row(b1)),
                     (R_FB, 6, fbias), (R_FG, 3, ln_g), (R_FBETA, 3, ln_b), (R_LG, 1, row(lg1)),
                     (R_LB, 1, row(lb1)), (R_GATE, 8, gate_w), (R_MASK, 8, mask.rearrange("(t b) s -> t (b s)", b=2))]
            for r, n, src in stack:
                sp.dma_start(PR[r:r + n, :], src).then_inc(ld["pr"], 16)
            sp.dma_start(CX[:], ctx_in.rearrange("(t b) s d -> (b s) t d", b=2)).then_inc(ld["ctx"], 16)
            for i, w in enumerate((wq1, wk1, wv1)):
                sp.dma_start(wqkv1[:, i, :], w).then_inc(ld["l1"], 16)
            sp.dma_start(dw_sb[:], dense_w).then_inc(ld["l1"], 16)
            sp.dma_start(bcast[:, 0, :], lg1.partition_broadcast(128)).then_inc(ld["bcast"], 16)
            sp.dma_start(bcast[:, 1, :], lb1.partition_broadcast(128)).then_inc(ld["bcast"], 16)
            sp.dma_start(qw_sb[:], qw.rearrange("n o d -> o n d")).then_inc(ld["q"], 16)
            sp.dma_start(sc_sb[:], scales.rearrange("n o g -> o n g")).then_inc(ld["q"], 16)
            sp.dma_start(la_sb[:], lora_a.rearrange("n r d -> r n d")).then_inc(ld["q"], 16)
            sp.dma_start(lb_sb[:], lora_b.rearrange("n o r -> o n r")).then_inc(ld["q"], 16)
            for j, src in enumerate((b2, fbias[0], fbias[2], fbias[4], fbias[5], dense_b)):
                sp.dma_start(rows[j:j + 1, :], row(src)).then_inc(ld["rows"], 16)
            sp.dma_start(w1_sb[:].rearrange("p c d -> p (c d)"), W1).then_inc(ld["mlp"], 16)
            sp.dma_start(w2_sb[:], W2.rearrange("(c p) d -> p c d", p=128)).then_inc(ld["mlp"], 16)
            sp.dma_start(gts[:, 0:2], g_xattn.partition_broadcast(128)).then_inc(ld["gates"], 16)
            sp.dma_start(gts[:, 2:4], g_ffn.partition_broadcast(128)).then_inc(ld["gates"], 16)

            sp.wait_ge(M["rows_split"], 1)
            for k in range(3):
                sp.dma_start(rows_b[k:k + 1, :, :], rows_p[:, k, :]).then_inc(ld["rows_b"], 16)

            def load_w1(e, slot):
                sp.dma_start(ew1[:, slot, :], w1s[e]).then_inc(ld_w1[slot], 16)

            def load_w2(e, slot):
                sp.dma_start(ew2[:, slot, 0:2, :], w2s[e][0:256, :].rearrange("(c p) d -> p c d", p=128)).then_inc(ld_w2[slot], 16)
                sp.dma_start(ew2[0:96, slot, 2, :], w2s[e][256:352, :]).then_inc(ld_w2[slot], 16)

            for e in range(2):
                load_w1(e, e)
                load_w2(e, e)
            for hf in range(2):
                with sp.Fori(1 - hf, E // 2) as i:
                    for slot in range(2):
                        sp.wait_ge(F["h"], 6 * i + (3 * slot + 3 * E * hf - 3))
                        load_w1(2 * i + slot, slot)
                        sp.wait_ge(F["oe"], 2 * i + (slot + E * hf - 1))
                        load_w2(2 * i + slot, slot)
            ov = out.rearrange("(t b) s d -> (b s) t d", b=2)
            for hf in range(2):
                sp.wait_ge(M["oe_read"], E * (hf + 1))
                sp.dma_start(ov[:, HT * hf:HT * hf + HT, :], X[:, HT * hf:HT * hf + HT, :]).then_inc(stored, 16)
            sp.wait_ge(stored, 32)

        @block.gpsimd
        def _(pool):
            g = nc.gpsimd
            n = [0]

            def link(ins):
                n[0] += 1
                ins.then_inc(pool_step, 1)
                pool.wait_ge(pool_step, n[0])

            def rstd_of(*step):
                i = LN_STEPS.index(step)
                pool.wait_ge(M["ln_var"], i + 1)
                link(g.tensor_scalar(ve[:, i, :], mv[:, i, :, 1], 1e-6 if LN_SMALL[i] else 1e-5, 1.0, ALU.add, ALU.mult))
                g.tensor_tensor(rstd[:, i, :], ve[:, i, :], neghalf[:], ALU.pow).then_inc(M["ln_rstd"], 1)

            g.memset(ident[:], 0.0)
            g.memset(hm[:], 1.0)
            link(g.memset(neghalf[:], -0.5))
            link(g.affine_select(out=ident[:], in_=ident[:], compare_op=ALU.not_equal, fill=1.0, base=0,
                                 pattern=[[-1, 128]], channel_multiplier=1))
            link(g.affine_select(out=hm[:], in_=hm[:], compare_op=ALU.is_ge, fill=0.0, base=0,
                                 pattern=[[-HD, NH]], channel_multiplier=1))
            link(g.affine_select(out=hm[:], in_=hm[:], compare_op=ALU.is_ge, fill=0.0, base=HD - 1,
                                 pattern=[[HD, NH]], channel_multiplier=-1))
            g.engine_nop().then_inc(hm_ready, 1)

            def x1(hf):
                rstd_of("x1", hf)
                if hf == 0:
                    g.memset(causal[:], 0.0)
                    g.memset(ones[:], 1.0)
                    g.memset(hmT[:], 1.0)
                    g.memset(par[:], 1.0)
                    g.memset(vx[:], 1.0)
                    link(g.memset(identb[:], 0.0))
                    g.affine_select(out=identb[:], in_=identb[:], compare_op=ALU.not_equal, fill=1.0, base=0,
                                    pattern=[[-1, 128]], channel_multiplier=1)
                    pv = par[:].rearrange("p (g two) d -> p g two d", two=2)
                    link(g.memset(pv[0:64, :, 1, :], 0.0))
                    link(g.memset(pv[64:128, :, 0, :], 0.0))
                    link(g.affine_select(out=hmT[:], in_=hmT[:], compare_op=ALU.is_ge, fill=0.0, base=0,
                                         pattern=[[1, 128]], channel_multiplier=-HD))
                    link(g.affine_select(out=hmT[:], in_=hmT[:], compare_op=ALU.is_ge, fill=0.0, base=HD - 1,
                                         pattern=[[-1, 128]], channel_multiplier=HD))
                    for b in range(2):
                        c = causal[64 * b:64 * b + 64, :, :]
                        link(g.affine_select(out=c, in_=c, compare_op=ALU.is_gt, fill=NEG, base=0,
                                             pattern=[[0, 8], [-1, S]], channel_multiplier=1))
                        link(g.memset(causal[64 * b:64 * b + 1, :, 0:1], 0.0))
                    g.iota(iota8[:], [[1, 8]], base=0, channel_multiplier=0,
                           allow_small_or_imprecise_dtypes=True).then_inc(consts, 1)

            def K(t):
                place_keys(pool, g, t, 1)

            def ctx_side(src, name, hf):
                def b_(c):
                    return bcast[:, c, :].unsqueeze(1).to_broadcast([128, HT, D])
                tl = src[:, HT * hf:HT * hf + HT, :]
                pool.wait_ge(ld["bcast"], 32)
                pool.wait_ge(M[name], hf + 1)
                link(g.tensor_tensor(tl, tl, b_(0), ALU.mult))
                link(g.tensor_tensor(tl, tl, b_(1), ALU.add))
                if name == "kn":
                    link(g.tensor_scalar(tl, tl, 0.0, 1e-6, ALU.max, ALU.add))
                for t in range(HT * hf, HT * hf + HT):
                    ins = g.tensor_scalar(kp[:, t, :] if name == "kn" else vx[:, t, 0:D], src[:, t, :],
                                          PC[:, R_MASK + t:R_MASK + t + 1], None, ALU.mult)
                ins.then_inc(M["kp_sb" if name == "kn" else "vx_sb"], 1)

            def split_rows():
                pool.wait_ge(ld["rows"], 16 * 6)
                link(g.tensor_copy(rows_p[:, 0], rows[:]))
                link(g.tensor_tensor(rows_r[:, 0], rows[:], rows_p[:, 0], ALU.subtract))
                link(g.tensor_copy(rows_p[:, 1], rows_r[:, 0]))
                link(g.tensor_tensor(rows_r[:, 1], rows_r[:, 0], rows_p[:, 1], ALU.subtract))
                g.tensor_copy(rows_p[:, 2], rows_r[:, 1]).then_inc(M["rows_split"], 1)

            def scaled_rows():
                pool.wait_ge(M["tanh_sb"], 1)
                pool.wait_ge(ld["bcast"], 32)
                link(g.tensor_scalar(gated_gb[:], bcast[:], tg[:, 1:2], None, ALU.mult))

            def add_beta(hf):
                pool.wait_ge(M["z_sb"], nth("z", hf, 2) + 1)
                tl = X[:, HT * hf:HT * hf + HT, :]
                g.tensor_tensor(XB[:, HT * hf:HT * hf + HT, :], tl, gated_gb[:, 1, :].unsqueeze(1).to_broadcast([128, HT, D]),
                                ALU.add).then_inc(M["xb"], 1)

            for name, *args in ORDER:
                if name == "x1":
                    x1(*args)
                elif name == "KP":
                    K(*args)
                elif name == "k1a":
                    ctx_side(kn, "kn", *args)
                elif name == "v1a":
                    ctx_side(vn, "vn", *args)
                elif name == "rows":
                    split_rows()
                elif (name, *args) in LN_STEPS:
                    rstd_of(name, *args)
                    if name == "down" and args[0] == 0:
                        scaled_rows()
                elif name == "beta":
                    add_beta(*args)

        @block.tensor
        def _(pe):
            def transposes(bank, src, out_sem):
                for t in range(HT):
                    last = pe.transpose(ps[:, bank, 128 * t:128 * t + 128], src[:, t, :], ident[:])
                last.then_inc(out_sem, 1)

            def tiles(t, hf):
                return t[:, HT * hf:HT * hf + HT, :]

            def tokens_out(bank, srcT, weights, bias_row=None, extra=()):
                if bias_row is not None:
                    add_row(bank, bias_row)
                for t in range(HT):
                    o = ps[:, bank, 128 * t:128 * t + 128]
                    pairs = [(srcT[:, 128 * t:128 * t + 128], weights)] + [(a[:, 128 * t:128 * t + 128], b) for a, b in extra]
                    for k, (l, r) in enumerate(pairs):
                        last = pe.matmul(o, l, r, start=(k == 0 and bias_row is None),
                                         stop=(k == len(pairs) - 1 and (bias_row is None or t == HT - 1)))
                return last

            def add_row(bank, i):
                pe.matmul(ps[:, bank, :], ones[:], rows_b[:, i, :].unsqueeze(1).to_broadcast([3, HT, D]), start=True, stop=False)

            def params():
                pe.wait_ge(pool_step, 2)
                pe.wait_ge(ld["pr"], 16 * 11)
                pe.transpose(ps[:, 7, 0:R_END], PR[:, :], ident[0:R_END, 0:R_END]).then_inc(F["params"], 1)

            def x1(hf):
                pe.wait_ge(M["x1"], hf + 1)
                transposes((0, 5)[hf], tiles(XN, hf), F["x1T"])

            def kq(hf):
                pe.wait_ge(ld["wkqv"], 48)
                pe.wait_ge(M["x1T_sb"], hf + 1)
                if hf == 1:
                    pe.wait_ge(M["vm_sb"], 3)
                pe.matmul(ps[:, (1, 6)[hf], :], wkqv[:, 0, :], XT[:, hf, :], start=True, stop=True).then_inc(F["k"], 1)
                pe.matmul(ps[:, (2, 7)[hf], :], wkqv[:, 1, :], XT[:, hf, :], start=True, stop=True).then_inc(F["q"], 1)

            def ctxT(hf):
                pe.wait_ge(ld["ctx"], 16)
                transposes(3 + hf, tiles(CX, hf), F["ctxT"])

            def values(c):
                pe.wait_ge(M["ctxT_sb"], c // 2 + 1)
                if c == 0:
                    pe.wait_ge(M["x1T_sb"], 2)
                if c == 2:
                    pe.wait_ge(M["params_sb"], 1)
                for b in range(4):
                    src = CT[:, c // 2, (4 * (c % 2) + b) * S:(4 * (c % 2) + b) * S + S]
                    for dup in range(2):
                        last = pe.matmul(ps[64 * dup:64 * dup + 64, (5, 6, 7, 3)[c], 128 * b:128 * b + 128], src,
                                         wkqv[:, 2, :], start=True, stop=True)
                last.then_inc(F["v"], 1)

            def lbT_():
                pe.wait_ge(ld["q"], 64)
                pe.wait_ge(M["k_sb"], 2)
                for n in range(6):
                    last = pe.transpose(ps[0:32, 5 + n // 4, 128 * (n % 4):128 * (n % 4) + 128], lb_sb[:, n, :], ident[:])
                last.then_inc(F["lbT"], 1)

            def weT_():
                pe.wait_ge(M["lbT_sb"], 1)
                pe.wait_ge(M["wdq_sb"], 1)
                for n in range(6):
                    o = ps[:, 5 + n // 4, 128 * (n % 4):128 * (n % 4) + 128]
                    pe.matmul(o, wdq[:, n, :], ident[:], start=True, stop=False)
                    last = pe.matmul(o, la_sb[:, n, :], lbT[:, n, :], start=False, stop=True)
                last.then_inc(F["weT"], 1)

            def k1(hf):
                pe.wait_ge(ld["l1"], 64)
                if hf == 0:
                    pe.wait_ge(M["q_sb"], 2)
                else:
                    pe.wait_ge(M["vn"], 1)
                tokens_out(7, CT[:, hf, :], wqkv1[:, 1, :]).then_inc(F["k1"], 1)

            def v1(hf):
                pe.wait_ge(M["kn"], hf + 1)
                tokens_out(7, CT[:, hf, :], wqkv1[:, 2, :]).then_inc(F["v1"], 1)

            def kv(hf, g):
                pe.wait_ge(M["kp_sb"], hf + 1)
                pe.wait_ge(M["vx_sb"], hf + 1)
                pe.wait_ge(M["vn"], 2)
                if (hf, g) != (0, 0):
                    pe.wait_ge(M["kvx_sb"], 4 * hf + g)
                for k, b in enumerate(kv_batches(hf, g)):
                    h0 = 64 * (b % 2)
                    last = pe.matmul(ps[:, 7, 132 * k:132 * k + 130], kp[h0:h0 + 64, b // 2, :],
                                     vx[h0:h0 + 64, b // 2, 0:130], start=True, stop=True)
                last.then_inc(F["kv"], 1)

            def S_(t):
                hf = t // HT
                if t == 0:
                    pe.wait_ge(consts, 1)
                pe.wait_ge(M["q_sb"], hf + 1)
                pe.wait_ge(M["keys_lo"], t + 1)
                pe.wait_ge(M["keys_hi"], t + 1)
                if t > 0:
                    pe.wait_ge(M["centered"], t)
                for hb in range(2):
                    pe.matmul(ps[:, hb, :], identb[:], causal[:].rearrange("p a s -> p (a s)"), start=True, stop=False)
                    for b in range(2):
                        tok = t * 128 + 64 * b
                        last = pe.matmul(ps[64 * b:64 * b + 64, hb, :], qT[:, hf, tok % HALF:tok % HALF + S],
                                         Km[:, t % 2, 8 * hb:8 * hb + 8, S * b:S * b + S], start=False, stop=True)
                last.then_inc(F["scores"], 1)

            def T1(t):
                pe.wait_ge(M["exped"], t + 1)
                for gq in range(2):
                    n = 2 * t + gq
                    if n >= 2:
                        pe.wait_ge(M["probsT_sb"], n - 1)
                    else:
                        pe.wait_ge(M["vm_sb"], 4)
                    for k in range(4):
                        pr = 4 * gq + k
                        last = pe.transpose(ps[:, 2 + gq, 128 * k:128 * k + 128],
                                            P[:, t % 2, 2 * pr:2 * pr + 2, :].rearrange("p a s -> p (a s)"), ident[:])
                    last.then_inc(F["probsT"], 1)

            def T2(t):
                pe.wait_ge(M["sums"], t + 1)
                if t > 0:
                    pe.wait_ge(M["heads_sb"], t)
                pe.transpose(ps[0:NH, 4, 0:128], rc[:, t % 2, :], ident[:]).then_inc(F["recT"], 1)

            def T3(t):
                pe.wait_ge(M["recT_sb"], t + 1)
                pe.matmul(ps[:, 4, 128:256], hmT[:], rT[:, t % 2, :], start=True, stop=True)
                pe.wait_ge(M["probsT_sb"], 2 * t + 2)
                for b in range(2):
                    for r in range(4):
                        last = pe.matmul(ps[32 * r:32 * r + 32, 4, 256 + 128 * b:384 + 128 * b],
                                         Vm[:, 2 * t + b, 32 * r:32 * r + 32],
                                         PT[:, t % 2, 2 * r:2 * r + 2, 64 * b:64 * b + 64], start=True, stop=True)
                last.then_inc(F["heads"], 1)

            def up(hf):
                pe.wait_ge(ld["mlp"], 32)
                pe.wait_ge(M["AT_sb"], 4 * hf + 4)
                if hf == 0:
                    pe.wait_ge(M["weT_sb"], 1)
                for j in range(4):
                    if j >= 2:
                        pe.wait_ge(M["up_sb"], 4 * hf + j - 1)
                    pe.matmul(ps[:, dbank(hf, j % 2), :], w1_sb[:, j, :], AT[:, hf, :], start=True, stop=True).then_inc(F["up"], 1)

            def down(hf):
                pe.wait_ge(M["up_sb"], 4 * hf + 4)
                pe.wait_ge(ld["rows_b"], 16 * 3)
                add_row(dbank(hf, 0), 0)
                for t in range(HT):
                    o = ps[:, dbank(hf, 0), 128 * t:128 * t + 128]
                    for j in range(4):
                        last = pe.matmul(o, H1[:, j, 128 * t:128 * t + 128], w2_sb[:, j, :], start=False,
                                         stop=(j == 3 and t == HT - 1))
                last.then_inc(F["down"], 1)

            def x2T(hf):
                pe.wait_ge(M["x2"], hf + 1)
                transposes(dbank(hf, 1), tiles(XN, hf), F["x2T"])

            def y(hf, i):
                pe.wait_ge(M["z_sb" if i else "x2T_sb"], nth("z", hf, i - 1) + 1 if i else hf + 1)
                tokens_out(dbank(hf, 0), hT[:, hf, :], weT[:, 2 * i, :], 1 + i).then_inc(F["y"], 1)

            def yT(hf, i):
                pe.wait_ge(M["yn"], nth("yT", hf, i) + 1)
                transposes(dbank(hf, 1), tiles(YN, hf), F["yT"])

            def z(hf, i):
                pe.wait_ge(M["gT_sb"], nth("yT", hf, i) + 1)
                if i < 2:
                    pe.matmul(ps[:, dbank(hf, 0), :], weT[:, 2 * i + 1, :], gT[:, hf, :], start=True, stop=True).then_inc(F["z"], 1)
                else:
                    tokens_out(dbank(hf, 0), gT[:, hf, :], weT[:, 5, :], 4,
                               extra=[(hT[:, hf, :], ident[:])]).then_inc(F["z"], 1)

            def x3T(hf):
                pe.wait_ge(M["x3"], hf + 1)
                transposes(dbank(hf, 1), tiles(XN, hf), F["x3T"])

            def q1(hf):
                pe.wait_ge(M["x3T_sb"], hf + 1)
                tokens_out(dbank(hf, 0), XT[:, hf, :], wqkv1[:, 0, :]).then_inc(F["q1"], 1)

            def q1T(hf):
                pe.wait_ge(M["q1_read"], hf + 1)
                transposes(dbank(hf, 1), tiles(YN, hf), F["q1T"])

            def att(hf):
                pe.wait_ge(M["q1T_sb"], hf + 1)
                pe.wait_ge(M["kvx_sb"], 4 * hf + 4)
                for t in range(HT):
                    for b in range(2):
                        last = pe.matmul(ps[64 * b:64 * b + 64, dbank(hf, t // 2), 144 * (t % 2):144 * (t % 2) + 144],
                                         qT[:, hf, 128 * t + 64 * b:128 * t + 64 * b + 64],
                                         kvx[:, 8 * hf + 2 * t + b, :], start=True, stop=True)
                last.then_inc(F["att"], 1)

            def hE_(hf):
                pe.wait_ge(M["att_sb"], hf + 1)
                for e in range(HD):
                    last = pe.transpose(ps[0:64, dbank(hf, e // 4), 128 * (e % 4):128 * (e % 4) + 128],
                                        AO[:, HT * hf:HT * hf + HT, e:D:HD], ident[:])
                last.then_inc(F["hE"], 1)

            def attT(hf):
                pe.wait_ge(M["hE_sb"], 2 * hf + 2)
                for m in range(8):
                    last = pe.transpose(ps[:, dbank(hf, 0), 64 * m:64 * m + 64], hE[:, hf, 16 * m:16 * m + 16, :], ident[0:64, 0:64])
                last.then_inc(F["attT"], 1)

            def dense(hf):
                pe.wait_ge(M["attT_sb"], hf + 1)
                tokens_out(dbank(hf, 1), AT[:, hf, :], dw_sb[:], 5).then_inc(F["dense"], 1)

            def x4T(hf):
                pe.wait_ge(M["x4"], hf + 1)
                transposes(dbank(hf, 0), tiles(XN, hf), F["x4T"])

            def gate(hf):
                pe.wait_ge(M["x4T_sb"], hf + 1)
                for t in range(HT):
                    last = pe.matmul(ps[:, dbank(hf, 1), 8 * t:8 * t + 8], XT[:, hf, 128 * t:128 * t + 128],
                                     PC[:, R_GATE:R_GATE + 8], start=True, stop=True)
                last.then_inc(F["gate"], 1)

            def chunk(c, slot, j, hf):
                k0, kn = KC[j]
                pe.wait_ge(M["act_sb"], c)
                for u in range(2):
                    mm = pe.matmul(ps[0:kn, PAIR[(slot + j) % 2][u], :], ew1[:, slot, u * INTER + k0:u * INTER + k0 + kn],
                                   XT[:, hf, :], start=True, stop=True)
                mm.then_inc(F["h"], 1)

            def products(slot, u):
                for t in (2 * u, 2 * u + 1):
                    for j, (k0, kn) in enumerate(KC):
                        last = pe.matmul(ps[:, 7, 128 * t:128 * t + 128], am[0:kn, slot, j, 128 * t:128 * t + 128],
                                         ew2[0:kn, slot, j, :], start=(j == 0), stop=(j == 2))
                return last

            def load_wait(r):
                return 16 * (r // 2 + 1)

            def C(c):
                r, j = c // 3, c % 3
                if c == 0:
                    pe.wait_ge(M["gate_read"], 1)
                    pe.wait_ge(M["kvx_sb"], 8)
                if j == 0:
                    pe.wait_ge(ld_w1[r % 2], load_wait(r))
                if c > 0:
                    chunk(c, r % 2, j, 0)
                else:
                    for u in range(2):
                        mm = pe.matmul(ps[:, PAIR[0][u], :], ew1[:, 0, u * INTER:u * INTER + 128], XT[:, 0, :], start=True, stop=True)
                    mm.then_inc(F["h"], 1)

            def P_(r, u):
                if u == 0:
                    pe.wait_ge(ld_w2[r % 2], 2 * load_wait(r))
                    pe.wait_ge(M["act_sb"], 3 * r + 4)
                    if r > 0:
                        pe.wait_ge(M["oe_read"], r)
                last = products(r % 2, u)
                if u == 1:
                    last.then_inc(F["oe"], 1)

            def later_round(r, slot, w1_loaded, w2_loaded):
                pe.wait_ge(ld_w1[slot], w1_loaded)
                chunk(3 * r, slot, 0, 1)
                pe.wait_ge(ld_w2[1 - slot], w2_loaded)
                pe.wait_ge(M["act_sb"], 3 * r + 1)
                pe.wait_ge(M["oe_read"], r - 1)
                products(1 - slot, 0)
                chunk(3 * r + 1, slot, 1, 1)
                products(1 - slot, 1).then_inc(F["oe"], 1)
                chunk(3 * r + 2, slot, 2, 1)

            def rounds():
                pe.wait_ge(M["x4T_sb"], 2)
                later_round(E, 0, load_wait(E), 2 * load_wait(E - 1))
                with pe.Fori(0, E // 2 - 1) as i:
                    later_round(2 * i + (E + 1), 1, 16 * i + load_wait(E + 1), 32 * i + 2 * load_wait(E))
                    later_round(2 * i + (E + 2), 0, 16 * i + load_wait(E + 2), 32 * i + 2 * load_wait(E + 1))
                later_round(2 * E - 1, 1, load_wait(2 * E - 1), 2 * load_wait(2 * E - 2))
                P_(2 * E - 1, 0)
                P_(2 * E - 1, 1)

            STEPS = dict(params=params, x1=x1, kq=kq, ctxT=ctxT, v=values, S=S_, T1=T1, T2=T2, T3=T3, lbT=lbT_, weT=weT_, k1=k1, v1=v1, kv=kv,
                         up=up, down=down, x2T=x2T, y=y, yT=yT, z=z, x3T=x3T, q1=q1, q1T=q1T, att=att, hE=hE_,
                         attT=attT, dense=dense, x4T=x4T, gate=gate, C=C, P=P_, rounds=rounds)
            for name, *args in ORDER:
                if name in STEPS:
                    STEPS[name](*args)

        @block.scalar
        def _(act):
            a = nc.scalar

            def evacuate(dst, src, want, count, done):
                act.wait_ge(F[want], count)
                a.copy(dst, src).then_inc(M[done], 1)

            def ctxT(hf):
                evacuate(CT[:, hf, :], ps[:, 3 + hf, :], "ctxT", hf + 1, "ctxT_sb")

            def x1(hf):
                evacuate(XT[:, hf, :], ps[:, (0, 5)[hf], :], "x1T", hf + 1, "x1T_sb")

            def kq(hf):
                act.wait_ge(M["params_sb"], 1)
                act.wait_ge(F["k"], hf + 1)
                a.activation(kT[:, hf, :], ps[:, (1, 6)[hf], :], ACT.Identity, bias=PC[:, R_BK:R_BK + 1]).then_inc(M["k_sb"], 1)
                act.wait_ge(F["q"], hf + 1)
                a.activation(qT[:, hf, :], ps[:, (2, 7)[hf], :], ACT.Identity, bias=PC[:, R_BQ:R_BQ + 1]).then_inc(M["q_sb"], 1)

            def fold(dst, src, want, done):
                act.wait_ge(F[want], 1)
                a.copy(dst[:, 0:4, :].rearrange("p n d -> p (n d)"), src[:, 5, :])
                a.copy(dst[:, 4:6, :].rearrange("p n d -> p (n d)"), src[:, 6, 0:256]).then_inc(M[done], 1)

            def lbT_():
                fold(lbT, ps[0:32], "lbT", "lbT_sb")

            def weT_():
                fold(weT, ps, "weT", "weT_sb")

            def S_(t):
                act.wait_ge(M["centered"], t + 1)
                a.activation(P[:, t % 2], P[:, t % 2], ACT.Exp).then_inc(M["exped"], 1)

            def T1(t):
                for gq in range(2):
                    n = 2 * t + gq
                    if t > 1:
                        act.wait_ge(F["heads"], t - 1)
                    evacuate(PT[:, t % 2, 4 * gq:4 * gq + 4, :].rearrange("p n q -> p (n q)"), ps[:, 2 + gq, :],
                             "probsT", n + 1, "probsT_sb")

            def T3(t):
                act.wait_ge(M["heads_sb"], t + 1)
                a.activation(AT[:, t // HT, 128 * (t % HT):128 * (t % HT) + 128], o2[:, t % 2].rearrange("p b s -> p (b s)"),
                             ACT.Identity, bias=PC[:, R_BV:R_BV + 1]).then_inc(M["AT_sb"], 1)

            def up(hf):
                if hf == 1:
                    act.wait_ge(F["down"], 1)
                for j in range(4):
                    act.wait_ge(F["up"], 4 * hf + j + 1)
                    a.activation(H1[:, j, :], ps[:, dbank(hf, j % 2), :], ACT.Gelu,
                                 bias=PC[:, R_B1 + j:R_B1 + j + 1]).then_inc(M["up_sb"], 1)

            def down(hf):
                if hf == 0:
                    act.wait_ge(ld["gates"], 32)
                    a.activation(tg[:], gts[:], ACT.Tanh).then_inc(M["tanh_sb"], 1)

            def x2T(hf):
                evacuate(hT[:, hf, :], ps[:, dbank(hf, 1), :], "x2T", hf + 1, "x2T_sb")

            def yT(hf, i):
                act.wait_ge(F["yT"], nth("yT", hf, i) + 1)
                a.activation(gT[:, hf, :], ps[:, dbank(hf, 1), :], ACT.Gelu, bias=PC[:, R_FBETA + i:R_FBETA + i + 1],
                             scale=PC[:, R_FG + i:R_FG + i + 1]).then_inc(M["gT_sb"], 1)

            def x3T(hf):
                evacuate(XT[:, hf, :], ps[:, dbank(hf, 1), :], "x3T", hf + 1, "x3T_sb")

            def q1T(hf):
                act.wait_ge(F["q1T"], hf + 1)
                a.activation(kT[:, hf, :], ps[:, dbank(hf, 1), :], ACT.Relu, bias=PC[:, R_LB:R_LB + 1],
                             scale=PC[:, R_LG:R_LG + 1]).then_inc(M["relu_sb"], 1)

            def hE_(hf):
                act.wait_ge(F["hE"], hf + 1)
                for u in range(2):
                    a.copy(hE[:, hf, :, 4 * u:4 * u + 4].rearrange("p n e -> p e n"),
                           ps[0:64, dbank(hf, u), :].rearrange("p (e n) -> p e n", e=4)).then_inc(M["hE_sb"], 1)

            def attT(hf):
                act.wait_ge(F["attT"], hf + 1)
                for b in range(2):
                    last = a.copy(AT[:, hf, :].rearrange("c (t b h q) -> c b q t h", t=HT, b=2, h=NH)[:, b],
                                  ps[:, dbank(hf, 0), 256 * b:256 * b + 256].rearrange("c (q t h) -> c q t h", q=4, t=HT))
                last.then_inc(M["attT_sb"], 1)

            def x4T(hf):
                evacuate(XT[:, hf, :], ps[:, dbank(hf, 0), :], "x4T", hf + 1, "x4T_sb")

            def route(hf):
                act.wait_ge(M["dlog"], hf + 1)
                a.activation(el[:, HT * hf:HT * hf + HT], dl[:, HT * hf:HT * hf + HT], ACT.Exp).then_inc(M["el_sb"], 1)

            def silu(c, par_, j, first=False):
                kn = KC[j][1]
                act.wait_ge(F["h"], c + 1)
                if not first:
                    act.wait_ge(M["act_sb"], c)
                a.activation(sg[0:kn, par_, :], ps[0:kn, PAIR[par_][0], :], ACT.Silu).then_inc(M["silu"], 1)

            def C(c):
                silu(c, c % 2, c % 3, c == 0)

            def rounds():
                with act.Fori(0, E // 2) as i:
                    for slot in range(2):
                        for j in range(3):
                            silu(6 * i + (3 * E + 3 * slot + j), (3 * slot + j) % 2, j)

            STEPS = dict(ctxT=ctxT, x1=x1, kq=kq, lbT=lbT_, weT=weT_, M=S_, T1=T1, T3=T3, up=up, down=down, x2T=x2T, yT=yT, x3T=x3T,
                         q1T=q1T, hE=hE_, attT=attT, x4T=x4T, route=route, C=C, rounds=rounds)
            for name, *args in ORDER:
                if name in STEPS:
                    STEPS[name](*args)

        @block.vector
        def _(dve):
            v = nc.vector
            n = [0]
            ln = [0]

            def link(ins):
                n[0] += 1
                ins.then_inc(dve_step, 1)
                dve.wait_ge(dve_step, n[0])

            def stats(src):
                for t in range(HT):
                    ins = v.bn_stats(bst[:, t, :], src[:, t, :])
                link(ins)
                for t in range(HT):
                    ins = v.bn_aggr(mv[:, ln[0], t, :], bst[:, t, :])
                ins.then_inc(M["ln_var"], 1)
                ln[0] += 1
                dve.wait_ge(M["ln_var"], ln[0])
                return ln[0] - 1

            def normalize(i, src, dst):
                dve.wait_ge(M["ln_rstd"], i + 1)
                for t in range(HT):
                    ins = v.tensor_scalar(dst[:, t, :], src[:, t, :], mv[:, i, t, 0:1], rstd[:, i, t:t + 1],
                                          ALU.subtract, ALU.mult)
                return ins

            def tiles(t, hf):
                return t[:, HT * hf:HT * hf + HT, :]

            def flat(t, hf):
                return tiles(t, hf).rearrange("p t d -> p (t d)")

            def bank(b):
                return ps[:, b, :].rearrange("p (t d) -> p t d", t=HT)

            ids = {}

            def params():
                v.engine_nop().then_inc(M["act_sb"], 1)
                dve.wait_ge(F["params"], 1)
                v.tensor_copy(PC[:], ps[:, 7, 0:R_END]).then_inc(M["params_sb"], 1)

            def x1(hf):
                dve.wait_ge(ld_x[hf], 16)
                i = stats(tiles(X, hf))
                normalize(i, tiles(X, hf), tiles(XN, hf)).then_inc(M["x1"], 1)

            def K(t):
                if t == 0:
                    dve.wait_ge(hm_ready, 1)
                place_keys(dve, v, t, 0)

            def values(c):
                if c == 0:
                    dve.wait_ge(consts, 1)
                dve.wait_ge(F["v"], c + 1)
                v.tensor_tensor(Vm[:, 4 * c:4 * c + 4, :], ps[:, (5, 6, 7, 3)[c], :].rearrange("p (b d) -> p b d", b=4),
                                par[:].rearrange("p h d -> p (h d)").unsqueeze(1).to_broadcast([128, 4, 128]),
                                ALU.mult).then_inc(M["vm_sb"], 1)
                if c == 3:
                    v.tensor_copy(blk[:], hm[:].unsqueeze(2).to_broadcast([128, NH, HD]))
                    link(v.tensor_reduce(pairsel[:, 0:2], hm[:].rearrange("p (r s j) -> p s r j", r=4, s=2), axis=AX.XY, op=ALU.add))

            def weights():
                dve.wait_ge(ld["q"], 64)
                link(v.tensor_copy(wf, qw_sb[:]))
                link(v.tensor_scalar(wf, wf, 1.0 / 7.5, -1.0, ALU.mult, ALU.add))
                v.tensor_tensor(wdq[:].rearrange("p n (g k) -> p (n g) k", g=8),
                                wf.rearrange("p n (g k) -> p (n g) k", g=8),
                                sc_sb[:].rearrange("p n g -> p (n g)").unsqueeze(2).to_broadcast([128, 48, 16]),
                                ALU.mult).then_inc(M["wdq_sb"], 1)

            def k1(hf):
                dve.wait_ge(F["k1"], hf + 1)
                ids["k", hf] = stats(bank(7))

            def k1n(hf):
                normalize(ids["k", hf], bank(7), tiles(kn, hf)).then_inc(M["kn"], 1)

            def v1(hf):
                dve.wait_ge(F["v1"], hf + 1)
                ids["v", hf] = stats(bank(7))

            def v1n(hf):
                normalize(ids["v", hf], bank(7), tiles(vn, hf)).then_inc(M["vn"], 1)

            def kv(hf, g):
                dve.wait_ge(F["kv"], 4 * hf + g + 1)
                bs = kv_batches(hf, g)
                nb = len(bs)
                kvb = ps[:, 7, 0:132 * nb].rearrange("p (b d) -> p b d", b=nb)
                v.tensor_tensor(kvx[:, bs[0]:bs[-1] + 1:2, 0:D], kvb[:, :, 0:D],
                                blk[:].rearrange("p h d -> p (h d)").unsqueeze(1).to_broadcast([128, nb, D]), ALU.mult)
                for b in range(nb):
                    ins = v.tensor_scalar(kvx[:, bs[b], D:D + NH], hm[:], kvb[:, b, D:D + 1], None, ALU.mult)
                ins.then_inc(M["kvx_sb"], 1)

            def S_(t):
                sc = ps[:, 0:2, :].rearrange("p u (h s) -> p (u h) s", s=S)
                dve.wait_ge(F["scores"], t + 1)
                link(v.tensor_reduce(mx[:, t % 2, :], sc, axis=AX.X, op=ALU.max))
                if t > 1:
                    dve.wait_ge(F["probsT"], 2 * t - 2)
                    dve.wait_ge(M["sums"], t - 1)
                v.tensor_tensor(P[:, t % 2], sc, mx[:, t % 2, :].unsqueeze(2).to_broadcast([128, NH, S]),
                                ALU.subtract).then_inc(M["centered"], 1)

            def T1(t):
                s = t % 2
                dve.wait_ge(M["exped"], t + 1)
                link(v.tensor_reduce(sm[:, s, :], P[:, s], axis=AX.X, op=ALU.add))
                if t > 1:
                    dve.wait_ge(F["recT"], t - 1)
                v.reciprocal(rc[:, s, :], sm[:, s, :]).then_inc(M["sums"], 1)

            def T2(t):
                s = t % 2
                dve.wait_ge(F["recT"], t + 1)
                v.tensor_copy(rT[:, s, :], ps[0:NH, 4, 0:128]).then_inc(M["recT_sb"], 1)

            def T3(t):
                s = t % 2
                dve.wait_ge(F["heads"], t + 1)
                if t > 1:
                    dve.wait_ge(M["AT_sb"], t - 1)
                    dve.wait_ge(M["heads_sb"], t - 1)
                ob = ps[:, 4, 256:512].rearrange("p (b j q) -> p b j q", b=2, j=2)
                link(v.tensor_scalar(o0[:, s], ob[:, :, 0, :], pairsel[:, 0:1], None, ALU.mult))
                link(v.scalar_tensor_tensor(o1[:, s], ob[:, :, 1, :], pairsel[:, 1:2], o0[:, s], ALU.mult, ALU.add))
                v.tensor_tensor(o2[:, s].rearrange("p b s -> p (b s)"), o1[:, s].rearrange("p b s -> p (b s)"),
                                ps[:, 4, 128:256], ALU.mult).then_inc(M["heads_sb"], 1)

            def add_gated(g, b, hf):
                link(v.scalar_tensor_tensor(flat(X, hf), ps[:, b, :], tg[:, g:g + 1], flat(X, hf), ALU.mult, ALU.add))

            def down(hf):
                dve.wait_ge(M["tanh_sb"], 1)
                dve.wait_ge(F["down"], hf + 1)
                add_gated(0, dbank(hf, 0), hf)
                ids[hf] = stats(tiles(X, hf))

            def x2T(hf):
                normalize(ids[hf], tiles(X, hf), tiles(XN, hf)).then_inc(M["x2"], 1)

            def y(hf, i):
                dve.wait_ge(F["y"], nth("y", hf, i) + 1)
                ids[hf] = stats(bank(dbank(hf, 0)))

            def yT(hf, i):
                normalize(ids[hf], bank(dbank(hf, 0)), tiles(YN, hf)).then_inc(M["yn"], 1)

            def z(hf, i):
                dve.wait_ge(F["z"], nth("z", hf, i) + 1)
                if i < 2:
                    v.scalar_tensor_tensor(hT[:, hf, :], ps[:, dbank(hf, 0), :], PC[:, R_FB + 2 * i + 1:R_FB + 2 * i + 2],
                                           hT[:, hf, :], ALU.add, ALU.add).then_inc(M["z_sb"], 1)
                else:
                    v.scalar_tensor_tensor(flat(X, hf), ps[:, dbank(hf, 0), :], tg[:, 2:3], flat(X, hf),
                                           ALU.mult, ALU.add).then_inc(M["z_sb"], 1)
                    dve.wait_ge(M["z_sb"], nth("z", hf, i) + 1)
                    ids[hf] = stats(tiles(X, hf))

            def x3T(hf):
                normalize(ids[hf], tiles(X, hf), tiles(XN, hf)).then_inc(M["x3"], 1)

            def q1(hf):
                dve.wait_ge(F["q1"], hf + 1)
                ids[hf] = stats(bank(dbank(hf, 0)))

            def q1T(hf):
                normalize(ids[hf], bank(dbank(hf, 0)), tiles(YN, hf)).then_inc(M["q1_read"], 1)

            def q1e(hf):
                dve.wait_ge(M["relu_sb"], hf + 1)
                v.tensor_scalar(qT[:, hf, :], kT[:, hf, :], 1e-6, None, ALU.add).then_inc(M["q1T_sb"], 1)

            def att(hf):
                dve.wait_ge(F["att"], hf + 1)
                for u in range(2):
                    z_ = zz[:, 2 * hf + u]
                    av = ps[:, dbank(hf, u), 0:288].rearrange("p (t c) -> p t c", t=2)
                    link(v.tensor_scalar(z_, av[:, :, D:D + NH], 1e-6, None, ALU.add))
                    link(v.reciprocal(z_, z_))
                    ins = v.tensor_tensor(AO[:, HT * hf + 2 * u:HT * hf + 2 * u + 2, :].rearrange("p t (h d) -> p t h d", h=NH),
                                          av[:, :, 0:D].rearrange("p t (h d) -> p t h d", h=NH),
                                          z_.unsqueeze(3).to_broadcast([128, 2, NH, HD]), ALU.mult)
                ins.then_inc(M["att_sb"], 1)

            def dense(hf):
                dve.wait_ge(F["dense"], hf + 1)
                i = ids[hf] = stats(bank(dbank(hf, 1)))
                if hf == 0:
                    dve.wait_ge(M["xb"], 1)
                for t in range(HT):
                    ins = v.scalar_tensor_tensor(YN[:, HT * hf + t, :], ps[:, dbank(hf, 1), 128 * t:128 * t + 128],
                                                 mv[:, i, t, 0:1], gated_gb[:, 0, :], ALU.subtract, ALU.mult)
                ins.then_inc(M["dense_read"], 1)

            def X3(hf):
                dve.wait_ge(M["ln_rstd"], ids[hf] + 1)
                dve.wait_ge(M["xb"], hf + 1)
                dve.wait_ge(M["dense_read"], hf + 1)
                for t in range(HT * hf, HT * hf + HT):
                    ins = v.scalar_tensor_tensor(X[:, t, :], YN[:, t, :], rstd[:, ids[hf], t % HT:t % HT + 1], XB[:, t, :],
                                                 ALU.mult, ALU.add)
                link(ins)
                ids[hf] = stats(tiles(X, hf))

            def x4T(hf):
                normalize(ids[hf], tiles(X, hf), tiles(XN, hf)).then_inc(M["x4"], 1)

            def gate(hf):
                dve.wait_ge(F["gate"], hf + 1)
                v.tensor_copy(tiles(lg, hf), ps[:, dbank(hf, 1), 0:32].rearrange("p (t e) -> p t e", t=HT)).then_inc(M["gate_read"], 1)
                dve.wait_ge(M["gate_read"], hf + 1)
                ts = range(HT * hf, HT * hf + HT)
                for t in ts:
                    ins = v.max(top[:, t, :], lg[:, t, :])
                link(ins)
                h_ = slice(HT * hf, HT * hf + HT)
                v.tensor_tensor(dl[:, h_], top[:, h_, 1], top[:, h_, 0], ALU.subtract).then_inc(M["dlog"], 1)
                for t in ts:
                    ins = v.max_index(topi[:, t, :], top[:, t, :], lg[:, t, :])
                link(ins)
                link(v.tensor_copy(topf[:, h_, :], topi[:, h_, :]))

            def route(hf):
                h_ = slice(HT * hf, HT * hf + HT)
                dve.wait_ge(M["el_sb"], hf + 1)
                link(v.tensor_scalar(den[:, h_], el[:, h_], 1.0, None, ALU.add))
                link(v.reciprocal(tw[:, h_, 0], den[:, h_]))
                link(v.tensor_tensor(tw[:, h_, 1], tw[:, h_, 0], el[:, h_], ALU.mult))
                link(v.tensor_scalar(tw[:, h_, :], tw[:, h_, :], tg[:, 3:4], None, ALU.mult))
                for s in range(2):
                    link(v.tensor_tensor(oh[:, h_, s, :], iota8[:].unsqueeze(1).to_broadcast([128, HT, 8]),
                                         topf[:, h_, s:s + 1].to_broadcast([128, HT, 8]), ALU.is_equal))
                    link(v.tensor_tensor(oh[:, h_, s, :], oh[:, h_, s, :], tw[:, h_, s:s + 1].to_broadcast([128, HT, 8]), ALU.mult))
                link(v.tensor_tensor(wexp[:, h_, :], oh[:, h_, 0, :], oh[:, h_, 1, :], ALU.add))

            def gated(c, slot, j, par_):
                kn = KC[j][1]
                dve.wait_ge(M["silu"], c + 1)
                v.tensor_tensor(am[0:kn, slot, j, :], ps[0:kn, PAIR[par_][1], :], sg[0:kn, par_, :], ALU.mult).then_inc(M["act_sb"], 1)

            def add_round(r, slot, hf, first=False):
                dve.wait_ge(F["oe"], r + 1)
                if not first:
                    dve.wait_ge(M["oe_read"], r)
                for t in range(HT):
                    ins = v.scalar_tensor_tensor(X[:, HT * hf + t, :], ps[:, 7, 128 * t:128 * t + 128],
                                                 wcur[:, slot, t:t + 1], X[:, HT * hf + t, :], ALU.mult, ALU.add)
                ins.then_inc(M["oe_read"], 1)

            def G(c):
                r, j = c // 3, c % 3
                if j == 0:
                    if r >= 2:
                        dve.wait_ge(F["oe"], r - 1)
                        dve.wait_ge(M["oe_read"], r - 1)
                    v.tensor_copy(wcur[:, r % 2, :], wexp[:, 0:HT, r])
                gated(c, r % 2, j, c % 2)

            def A(r):
                add_round(r, r % 2, 0, r == 0)

            def later_round(r, slot, weights, hf):
                dve.wait_ge(F["oe"], r - 1)
                dve.wait_ge(M["oe_read"], r - 1)
                v.tensor_copy(wcur[:, slot, :].unsqueeze(2), weights)
                gated(3 * r, slot, 0, slot)
                gated(3 * r + 1, slot, 1, 1 - slot)
                add_round(r - 1, 1 - slot, hf)
                gated(3 * r + 2, slot, 2, slot)

            def rounds():
                later_round(E, 0, wexp[:, HT:T, 0:1], 0)
                with dve.Fori(0, E // 2 - 1) as i:
                    for k in range(2):
                        later_round(2 * i + (E + 1 + k), 1 - k, wexp[:, HT:T, bass.ds(2 * i + (1 + k), 1)], 1)
                later_round(2 * E - 1, 1, wexp[:, HT:T, E - 1:E], 1)
                add_round(2 * E - 1, 1, 1)

            STEPS = dict(params=params, x1=x1, v=values, weights=weights, k1=k1, v1=v1, k1n=k1n, v1n=v1n, kv=kv, M=S_, K=K, T1=T1, T2=T2, T3=T3, q1e=q1e, down=down, x2T=x2T,
                         y=y, yT=yT, z=z, x3T=x3T, q1=q1, q1T=q1T, att=att, dense=dense, X3=X3, x4T=x4T, gate=gate,
                         route=route, G=G, A=A, rounds=rounds)
            for name, *args in ORDER:
                if name in STEPS:
                    STEPS[name](*args)


_INS = ['x', 'ctx_1024', 'mask_BxS2_ff1', 'g_xattn', 'g_ffn', 'L0_xattn_Wk', 'L0_xattn_bk', 'L0_xattn_Wq', 'L0_xattn_bq',
        'L0_xattn_Wv', 'L0_xattn_bv', 'L0_xattn_W1', 'L0_xattn_b1', 'L0_xattn_W2', 'L0_xattn_b2', 'L0_ffn_qweights',
        'L0_ffn_scales', 'L0_ffn_biases', 'L0_ffn_lora_a', 'L0_ffn_lora_b', 'L0_ffn_ln_gamma', 'L0_ffn_ln_beta',
        'L1_xattn_wq', 'L1_xattn_wk', 'L1_xattn_wv', 'L1_xattn_ln_gamma', 'L1_xattn_ln_beta', 'L1_xattn_dense_w',
        'L1_xattn_dense_b', 'L1_ffn_gate_w', 'L1_ffn_w1_stacked', 'L1_ffn_w2_stacked']


def kernel(**inputs):
    import numpy as _np
    import concourse.bacc as _bacc
    from concourse import mybir as _mybir
    from concourse.bass_utils import run_bass_kernel_spmd as _run

    nc = _bacc.Bacc("TRN2", target_bir_lowering=False, num_devices=1)
    arrays, args = {}, []
    for name in _INS:
        a = _np.ascontiguousarray(inputs[name])
        arrays[f"in_{name}_dram"] = a
        args.append(nc.dram_tensor(f"in_{name}_dram", a.shape, _mybir.dt.from_np(a.dtype), kind="ExternalInput").ap())
    out = nc.dram_tensor("out_0_dram", (16, 64, 128), _mybir.dt.float32, kind="ExternalOutput").ap()
    flamingo(nc, *args, out)
    r = _run(nc, [arrays], core_ids=[0])
    return r.results[0]["out_0_dram"]
```

```python
from contextlib import ExitStack

import concourse.bass as bass
from concourse import mybir

ALU = mybir.AluOpType
ACT = mybir.ActivationFunctionType
AX = mybir.AxisListType
F32 = mybir.dt.float32
BF16 = mybir.dt.bfloat16
I32 = mybir.dt.int32
U32 = mybir.dt.uint32

D = 128
S = 64
T = 8
HT = 4
HALF = 512
NH = 16
HD = 8
E = 8
INTER = 352
KC = [(0, 128), (128, 128), (256, 96)]
NEG = -1.0e30

R_BK, R_BQ, R_BV, R_B1, R_FB, R_FG, R_FBETA, R_LG, R_LB, R_GATE, R_MASK, R_END = 0, 1, 2, 3, 7, 13, 16, 19, 20, 21, 29, 37


def kv_batches(hf, g):
    return [8 * hf + 2 * m + g % 2 for m in (range(3), [3])[g // 2]]


def down_chain(hf):
    ffn = [(n, hf, i) for i in range(3) for n in ("y", "yT", "z")]
    return [(n, hf) for n in ("up", "down", "x2T")] + ffn + [
        (n, hf) for n in ("x3T", "q1", "q1T", "att", "hE", "attT", "dense", "X3", "x4T", "gate", "route")]


ORDER = """
    x1.0 params kq.0 ctxT.0 x1.1 K.0 ctxT.1 KP.0 v.0 K.1 v.1 v.2 S.0 KP.1 kq.1 M.0 v.3 KP.2 k1.0 K.2 S.1 K.3 k1n.0
    M.1 v1.0 lbT KP.3 k1a.0.0 S.2 T1.0 v1n.0 M.2 k1.1 T2.0 v1a.0.0 T1.1 k1n.1 k1a.0.1 v1a.0.1 T3.0 weights v1a.0.3
    v1.1 T1.2 k1a.0.2 T2.1 S.3 KP.4 v1a.0.4 M.3 T3.1 weT T2.2 k1a.0.3 K.4 T1.3 T3.2 k1a.0.4 S.4 T2.3 T3.3 K.5 rows
    up.0 M.4 v1n.1 kv.0.0 down.0 KP.5 x2T.0 K.6 y.0.0 S.5 T1.4 yT.0.0 M.5 z.0.0 KP.6 kv.0.1 k1a.1.0 y.0.1 S.6
    v1a.1.0 yT.0.1 k1a.1.1 k1a.1.2 T1.5 K.7 z.0.1 kv.0.2 T2.4 y.0.2 T3.4 T2.5 k1a.1.3 v1a.1.1 yT.0.2 KP.7 M.6 T3.5
    z.0.2 S.7 T1.6 x3T.0 M.7 T2.6 q1.0 T3.6 T1.7 kv.0.3 T2.7 T3.7 k1a.1.4 up.1 q1T.0 q1e.0 down.1 att.0 x2T.1 y.1.0
    hE.0 beta.0 attT.0 yT.1.0 dense.0 v1a.1.3 z.1.0 X3.0 y.1.1 x4T.0 gate.0 v1a.1.4 yT.1.1 z.1.1 kv.1.0 y.1.2
    yT.1.2 kv.1.1 route.0 z.1.2 kv.1.2 kv.1.3 x3T.1 q1.1 C.0 C.1 q1T.1 G.0 q1e.1 att.1 beta.1 C.2 hE.1 G.1 G.2 C.3
    attT.1 dense.1 C.4 X3.1 P.0.0 P.0.1 G.3 G.4 C.5 x4T.1 G.5 A.0 C.6 gate.1 G.6 route.1 C.7 P.1.0 C.8 G.7 P.1.1
    G.8 A.1 C.9 G.9 C.10 P.2.0 G.10 P.2.1 C.11 A.2 G.11 C.12 C.13 G.12 C.14 P.3.0 P.3.1 G.13 G.14 A.3 C.15 G.15
    C.16 P.4.0 C.17 G.16 P.4.1 C.18 G.17 C.19 A.4 G.18 G.19 P.5.0 C.20 G.20 P.5.1 A.5 C.21 C.22 G.21 C.23 G.22
    P.6.0 P.6.1 G.23 A.6 rounds
"""
ORDER = [tuple(int(w) if w.isdigit() else w for w in step.split(".")) for step in ORDER.split()]


def nth(name, hf, i):
    return [s for s in ORDER if s[0] == name].index((name, hf, i))


PAIR = ((0, 1), (5, 6))
LN_STEPS = [s for s in ORDER if s[0] in ("x1", "k1", "v1", "down", "y", "q1", "dense", "X3") or (s[0] == "z" and s[2] == 2)]
LN_SMALL = [s[0] in ("k1", "v1", "q1", "dense") for s in LN_STEPS]


def flamingo(nc, x, ctx_in, mask, g_xattn, g_ffn, Wk, bk, Wq, bq, Wv, bv, W1, b1, W2, b2,
             qw, scales, fbias, lora_a, lora_b, ln_g, ln_b, wq1, wk1, wv1, lg1, lb1,
             dense_w, dense_b, gate_w, w1s, w2s, out):
    with ExitStack() as ctx:
        def sb(name, shape, dt=F32):
            return ctx.enter_context(nc.sbuf_tensor(name, shape, dt))

        def sem(name):
            return ctx.enter_context(nc.semaphore(name))

        ps = ctx.enter_context(nc.psum_tensor("ps", [128, 8, 512], F32))

        X = sb("X", [128, T, D])
        CX = sb("CX", [128, T, D])
        PR = sb("PR", [R_END, 128])
        PC = sb("PC", [128, R_END])
        wkqv = sb("wkqv", [128, 3, D])
        w1_sb = sb("w1_sb", [128, 4, D])
        w2_sb = sb("w2_sb", [128, 4, D])
        rows = sb("rows", [6, D])
        rows_p = sb("rows_p", [6, 3, D], BF16)
        rows_r = sb("rows_r", [6, 2, D])
        rows_b = sb("rows_b", [3, 6, D], BF16)
        bcast = sb("bcast", [128, 2, D])
        gated_gb = sb("gated_gb", [128, 2, D])
        gts = sb("gts", [128, 4])
        tg = sb("tg", [128, 4])
        qw_sb = sb("qw_sb", [128, 6, D], I32)
        sc_sb = sb("sc_sb", [128, 6, 8])
        la_sb = sb("la_sb", [32, 6, D])
        lb_sb = sb("lb_sb", [128, 6, 32])
        wqkv1 = sb("wqkv1", [128, 3, D])
        dw_sb = sb("dw_sb", [128, D])
        ew1 = sb("ew1", [128, 2, 2 * INTER])
        ew2 = sb("ew2", [128, 2, 3, D])

        ident = sb("ident", [128, 128])
        identb = sb("identb", [128, 128], BF16)
        causal = sb("causal", [128, 8, S], BF16)
        hm = sb("hm", [128, NH])
        hmT = sb("hmT", [NH, 128])
        blk = sb("blk", [128, NH, HD])
        par = sb("par", [128, NH, HD])
        pairsel = sb("pairsel", [128, 4])
        neghalf = sb("neghalf", [128, HT])
        ones = sb("ones", [3, 128], BF16)
        iota8 = sb("iota8", [128, 8])

        XN = sb("XN", [128, T, D])
        XT = sb("XT", [128, 2, HALF])
        CT = sb("CT", [128, 2, HALF])
        kT = sb("kT", [128, 2, HALF])
        qT = sb("qT", [128, 2, HALF])
        Km = sb("Km", [128, 2, NH, 128])
        Vm = sb("Vm", [128, 16, D])
        P = sb("P", [128, 2, NH, S])
        PT = sb("PT", [128, 2, 8, 128])
        mx = sb("mx", [128, 2, NH])
        sm = sb("sm", [128, 2, NH])
        rc = sb("rc", [128, 2, NH])
        rT = sb("rT", [NH, 2, 128])
        o0 = sb("o0", [128, 2, 2, S])
        o1 = sb("o1", [128, 2, 2, S])
        o2 = sb("o2", [128, 2, 2, S])
        AT = sb("AT", [128, 2, HALF])
        hE = P[0:64].rearrange("p a h s -> p (a h s)").rearrange("p (f n e) -> p f n e", f=2, e=HD)
        H1 = sb("H1", [128, 4, HALF])
        wdq = sb("wdq", [128, 6, D])
        wf = H1[:].rearrange("p c (a d) -> p (c a) d", d=D)[:, 0:6, :]
        lbT = sb("lbT", [32, 6, D])
        weT = sb("weT", [128, 6, D])
        hT = sb("hT", [128, 2, HALF])
        YN = sb("YN", [128, T, D])
        gT = AT
        XB = sb("XB", [128, T, D])
        kp = sb("kp", [128, T, D])
        vx = sb("vx", [128, T, 132])
        kvx = sb("kvx", [128, 16, 144])
        zz = sb("zz", [128, 4, 2, NH])
        AO = CX
        kn = sb("kn", [128, T, D])
        vn = sb("vn", [128, T, D])
        bst = sb("bst", [128, HT, 6])
        NLN = len(LN_SMALL)
        mv = sb("mv", [128, NLN, HT, 2])
        ve = sb("ve", [128, NLN, HT])
        rstd = sb("rstd", [128, NLN, HT])
        lg = sb("lg", [128, T, 8])
        top = sb("top", [128, T, 8])
        topi = sb("topi", [128, T, 8], U32)
        topf = sb("topf", [128, T, 8])
        dl = sb("dl", [128, T])
        el = sb("el", [128, T])
        den = sb("den", [128, T])
        tw = sb("tw", [128, T, 2])
        oh = sb("oh", [128, T, 2, 8])
        wexp = sb("wexp", [128, T, 8])
        wcur = sb("wcur", [128, 2, HT])
        sg = sb("sg", [128, 2, HALF])
        am = sb("am", [128, 2, 3, HALF])

        names = ["bcast", "rows_b", "ctx", "pr", "wkqv", "mlp", "rows", "gates", "q", "l1"]
        ld = {n: sem("ld_" + n) for n in names}
        ld_x = [sem("ld_x_0"), sem("ld_x_1")]
        ld_w1 = [sem("ld_expert_w1_even"), sem("ld_expert_w1_odd")]
        ld_w2 = [sem("ld_expert_w2_even"), sem("ld_expert_w2_odd")]
        stored = sem("stored")
        consts = sem("consts_ready")
        hm_ready = sem("head_mask_ready")
        pool_step = sem("pool_step")
        dve_step = sem("dve_step")
        F = {n: sem("pe_" + n) for n in [
            "params", "ctxT", "v", "x1T", "k", "q", "lbT", "weT", "k1", "v1", "kv", "scores", "probsT", "heads",
            "recT", "up", "down", "x2T", "y", "yT", "z", "x3T", "q1", "q1T", "att", "hE", "attT", "dense",
            "x4T", "gate", "h", "oe"]}
        M = {n: sem(n) for n in [
            "params_sb", "ctxT_sb", "vm_sb", "x1", "x1T_sb", "k_sb", "q_sb", "wdq_sb", "lbT_sb", "weT_sb",
            "kp_sb", "vx_sb", "kvx_sb", "centered", "exped", "sums", "probsT_sb", "recT_sb",
            "heads_sb", "AT_sb", "up_sb", "x2", "x2T_sb", "yn", "gT_sb", "z_sb", "x3",
            "x3T_sb", "q1_read", "q1T_sb", "relu_sb", "att_sb", "hE_sb", "attT_sb", "dense_read", "x4", "x4T_sb",
            "gate_read", "dlog", "el_sb", "silu", "act_sb", "oe_read", "tanh_sb",
            "ln_var", "ln_rstd", "keys_lo", "keys_hi", "kn", "vn", "rows_split", "xb"]}

        block = ctx.enter_context(nc.Block())

        def dbank(hf, k):
            return ((5, 6), (2, 3))[hf][k]

        def place_keys(eng, calls, t, part):
            hf, hs = t // HT, slice(8 * part, 8 * part + 8)
            eng.wait_ge(M["k_sb"], hf + 1)
            if t > 1:
                eng.wait_ge(F["scores"], t - 1)
            calls.tensor_tensor(Km[:, t % 2, hs, :],
                                kT[:, hf, 128 * (t % HT):128 * (t % HT) + 128].unsqueeze(1).to_broadcast([128, 8, 128]),
                                hm[:, hs].unsqueeze(2).to_broadcast([128, 8, 128]),
                                ALU.mult).then_inc(M[("keys_lo", "keys_hi")[part]], 1)

        @block.sync
        def _(sp):
            xv = x.rearrange("(t b) s d -> (b s) t d", b=2)
            row = lambda a: a.rearrange("(a d) -> a d", d=128)
            for hf in range(2):
                sp.dma_start(X[:, HT * hf:HT * hf + HT, :], xv[:, HT * hf:HT * hf + HT, :]).then_inc(ld_x[hf], 16)
            for i, w in enumerate((Wk, Wq, Wv)):
                sp.dma_start(wkqv[:, i, :], w).then_inc(ld["wkqv"], 16)
            stack = [(R_BK, 1, row(bk)), (R_BQ, 1, row(bq)), (R_BV, 1, row(bv)), (R_B1, 4, row(b1)),
                     (R_FB, 6, fbias), (R_FG, 3, ln_g), (R_FBETA, 3, ln_b), (R_LG, 1, row(lg1)),
                     (R_LB, 1, row(lb1)), (R_GATE, 8, gate_w), (R_MASK, 8, mask.rearrange("(t b) s -> t (b s)", b=2))]
            for r, n, src in stack:
                sp.dma_start(PR[r:r + n, :], src).then_inc(ld["pr"], 16)
            sp.dma_start(CX[:], ctx_in.rearrange("(t b) s d -> (b s) t d", b=2)).then_inc(ld["ctx"], 16)
            for i, w in enumerate((wq1, wk1, wv1)):
                sp.dma_start(wqkv1[:, i, :], w).then_inc(ld["l1"], 16)
            sp.dma_start(dw_sb[:], dense_w).then_inc(ld["l1"], 16)
            sp.dma_start(bcast[:, 0, :], lg1.partition_broadcast(128)).then_inc(ld["bcast"], 16)
            sp.dma_start(bcast[:, 1, :], lb1.partition_broadcast(128)).then_inc(ld["bcast"], 16)
            sp.dma_start(qw_sb[:], qw.rearrange("n o d -> o n d")).then_inc(ld["q"], 16)
            sp.dma_start(sc_sb[:], scales.rearrange("n o g -> o n g")).then_inc(ld["q"], 16)
            sp.dma_start(la_sb[:], lora_a.rearrange("n r d -> r n d")).then_inc(ld["q"], 16)
            sp.dma_start(lb_sb[:], lora_b.rearrange("n o r -> o n r")).then_inc(ld["q"], 16)
            for j, src in enumerate((b2, fbias[0], fbias[2], fbias[4], fbias[5], dense_b)):
                sp.dma_start(rows[j:j + 1, :], row(src)).then_inc(ld["rows"], 16)
            sp.dma_start(w1_sb[:].rearrange("p c d -> p (c d)"), W1).then_inc(ld["mlp"], 16)
            sp.dma_start(w2_sb[:], W2.rearrange("(c p) d -> p c d", p=128)).then_inc(ld["mlp"], 16)
            sp.dma_start(gts[:, 0:2], g_xattn.partition_broadcast(128)).then_inc(ld["gates"], 16)
            sp.dma_start(gts[:, 2:4], g_ffn.partition_broadcast(128)).then_inc(ld["gates"], 16)

            sp.wait_ge(M["rows_split"], 1)
            for k in range(3):
                sp.dma_start(rows_b[k:k + 1, :, :], rows_p[:, k, :]).then_inc(ld["rows_b"], 16)

            def load_w1(e, slot):
                sp.dma_start(ew1[:, slot, :], w1s[e]).then_inc(ld_w1[slot], 16)

            def load_w2(e, slot):
                sp.dma_start(ew2[:, slot, 0:2, :], w2s[e][0:256, :].rearrange("(c p) d -> p c d", p=128)).then_inc(ld_w2[slot], 16)
                sp.dma_start(ew2[0:96, slot, 2, :], w2s[e][256:352, :]).then_inc(ld_w2[slot], 16)

            for e in range(2):
                load_w1(e, e)
                load_w2(e, e)
            for hf in range(2):
                with sp.Fori(1 - hf, E // 2) as i:
                    for slot in range(2):
                        sp.wait_ge(F["h"], 6 * i + (3 * slot + 3 * E * hf - 3))
                        load_w1(2 * i + slot, slot)
                        sp.wait_ge(F["oe"], 2 * i + (slot + E * hf - 1))
                        load_w2(2 * i + slot, slot)
            ov = out.rearrange("(t b) s d -> (b s) t d", b=2)
            for hf in range(2):
                sp.wait_ge(M["oe_read"], E * (hf + 1))
                sp.dma_start(ov[:, HT * hf:HT * hf + HT, :], X[:, HT * hf:HT * hf + HT, :]).then_inc(stored, 16)
            sp.wait_ge(stored, 32)

        @block.gpsimd
        def _(pool):
            g = nc.gpsimd
            n = [0]

            def link(ins):
                n[0] += 1
                ins.then_inc(pool_step, 1)
                pool.wait_ge(pool_step, n[0])

            def rstd_of(*step):
                i = LN_STEPS.index(step)
                pool.wait_ge(M["ln_var"], i + 1)
                link(g.tensor_scalar(ve[:, i, :], mv[:, i, :, 1], 1e-6 if LN_SMALL[i] else 1e-5, 1.0, ALU.add, ALU.mult))
                g.tensor_tensor(rstd[:, i, :], ve[:, i, :], neghalf[:], ALU.pow).then_inc(M["ln_rstd"], 1)

            g.memset(ident[:], 0.0)
            g.memset(hm[:], 1.0)
            link(g.memset(neghalf[:], -0.5))
            link(g.affine_select(out=ident[:], in_=ident[:], compare_op=ALU.not_equal, fill=1.0, base=0,
                                 pattern=[[-1, 128]], channel_multiplier=1))
            link(g.affine_select(out=hm[:], in_=hm[:], compare_op=ALU.is_ge, fill=0.0, base=0,
                                 pattern=[[-HD, NH]], channel_multiplier=1))
            link(g.affine_select(out=hm[:], in_=hm[:], compare_op=ALU.is_ge, fill=0.0, base=HD - 1,
                                 pattern=[[HD, NH]], channel_multiplier=-1))
            g.engine_nop().then_inc(hm_ready, 1)

            def x1(hf):
                rstd_of("x1", hf)
                if hf == 0:
                    g.memset(causal[:], 0.0)
                    g.memset(ones[:], 1.0)
                    g.memset(hmT[:], 1.0)
                    g.memset(par[:], 1.0)
                    g.memset(vx[:], 1.0)
                    link(g.memset(identb[:], 0.0))
                    g.affine_select(out=identb[:], in_=identb[:], compare_op=ALU.not_equal, fill=1.0, base=0,
                                    pattern=[[-1, 128]], channel_multiplier=1)
                    pv = par[:].rearrange("p (g two) d -> p g two d", two=2)
                    link(g.memset(pv[0:64, :, 1, :], 0.0))
                    link(g.memset(pv[64:128, :, 0, :], 0.0))
                    link(g.affine_select(out=hmT[:], in_=hmT[:], compare_op=ALU.is_ge, fill=0.0, base=0,
                                         pattern=[[1, 128]], channel_multiplier=-HD))
                    link(g.affine_select(out=hmT[:], in_=hmT[:], compare_op=ALU.is_ge, fill=0.0, base=HD - 1,
                                         pattern=[[-1, 128]], channel_multiplier=HD))
                    for b in range(2):
                        c = causal[64 * b:64 * b + 64, :, :]
                        link(g.affine_select(out=c, in_=c, compare_op=ALU.is_gt, fill=NEG, base=0,
                                             pattern=[[0, 8], [-1, S]], channel_multiplier=1))
                        link(g.memset(causal[64 * b:64 * b + 1, :, 0:1], 0.0))
                    g.iota(iota8[:], [[1, 8]], base=0, channel_multiplier=0,
                           allow_small_or_imprecise_dtypes=True).then_inc(consts, 1)

            def K(t):
                place_keys(pool, g, t, 1)

            def ctx_side(src, name, hf, part):
                tl = src[:, HT * hf:HT * hf + HT, :]
                if part < 2:
                    if part == 0:
                        pool.wait_ge(ld["bcast"], 32)
                        pool.wait_ge(M[name], hf + 1)
                    link(g.tensor_tensor(tl, tl, bcast[:, part, :].unsqueeze(1).to_broadcast([128, HT, D]), (ALU.mult, ALU.add)[part]))
                elif part == 2:
                    if name == "kn":
                        link(g.tensor_scalar(tl, tl, 0.0, 1e-6, ALU.max, ALU.add))
                else:
                    for t in (HT * hf + 2 * part - 6, HT * hf + 2 * part - 5):
                        ins = g.tensor_scalar(kp[:, t, :] if name == "kn" else vx[:, t, 0:D], src[:, t, :],
                                              PC[:, R_MASK + t:R_MASK + t + 1], None, ALU.mult)
                    if part == 4:
                        ins.then_inc(M["kp_sb" if name == "kn" else "vx_sb"], 1)

            def split_rows():
                pool.wait_ge(ld["rows"], 16 * 6)
                link(g.tensor_copy(rows_p[:, 0], rows[:]))
                link(g.tensor_tensor(rows_r[:, 0], rows[:], rows_p[:, 0], ALU.subtract))
                link(g.tensor_copy(rows_p[:, 1], rows_r[:, 0]))
                link(g.tensor_tensor(rows_r[:, 1], rows_r[:, 0], rows_p[:, 1], ALU.subtract))
                g.tensor_copy(rows_p[:, 2], rows_r[:, 1]).then_inc(M["rows_split"], 1)

            def scaled_rows():
                pool.wait_ge(M["tanh_sb"], 1)
                pool.wait_ge(ld["bcast"], 32)
                link(g.tensor_scalar(gated_gb[:], bcast[:], tg[:, 1:2], None, ALU.mult))

            def add_beta(hf):
                pool.wait_ge(M["z_sb"], 2 * nth("z", hf, 2) + 2)
                tl = X[:, HT * hf:HT * hf + HT, :]
                g.tensor_tensor(XB[:, HT * hf:HT * hf + HT, :], tl, gated_gb[:, 1, :].unsqueeze(1).to_broadcast([128, HT, D]),
                                ALU.add).then_inc(M["xb"], 1)

            for name, *args in ORDER:
                if name == "x1":
                    x1(*args)
                elif name == "KP":
                    K(*args)
                elif name == "k1a":
                    ctx_side(kn, "kn", *args)
                elif name == "v1a":
                    ctx_side(vn, "vn", *args)
                elif name == "rows":
                    split_rows()
                elif (name, *args) in LN_STEPS:
                    rstd_of(name, *args)
                    if name == "down" and args[0] == 0:
                        scaled_rows()
                elif name == "beta":
                    add_beta(*args)

        @block.tensor
        def _(pe):
            def transposes(bank, src, out_sem, ready=None, n=0):
                for t in range(HT):
                    if ready is not None and t % 2 == 0:
                        pe.wait_ge(M[ready], 2 * n + t // 2 + 1)
                    last = pe.transpose(ps[:, bank, 128 * t:128 * t + 128], src[:, t, :], ident[:])
                last.then_inc(out_sem, 1)

            def tiles(t, hf):
                return t[:, HT * hf:HT * hf + HT, :]

            def tokens_out(bank, srcT, weights, done, bias_row=None, extra=(), ready=None, n=0):
                if bias_row is not None:
                    if ready is not None:
                        pe.wait_ge(M[ready], 2 * n + 1)
                    add_row(bank, bias_row)
                for t in range(HT):
                    if ready is not None and t % 2 == 0:
                        pe.wait_ge(M[ready], 2 * n + t // 2 + 1)
                    o = ps[:, bank, 128 * t:128 * t + 128]
                    pairs = [(srcT[:, 128 * t:128 * t + 128], weights)] + [(a[:, 128 * t:128 * t + 128], b) for a, b in extra]
                    for k, (l, r) in enumerate(pairs):
                        last = pe.matmul(o, l, r, start=(k == 0 and bias_row is None),
                                         stop=(k == len(pairs) - 1 and (bias_row is None or t == HT - 1)))
                last.then_inc(F[done], 1)

            def add_row(bank, i):
                pe.matmul(ps[:, bank, :], ones[:], rows_b[:, i, :].unsqueeze(1).to_broadcast([3, HT, D]), start=True, stop=False)

            def params():
                pe.wait_ge(pool_step, 2)
                pe.wait_ge(ld["pr"], 16 * 11)
                pe.transpose(ps[:, 7, 0:R_END], PR[:, :], ident[0:R_END, 0:R_END]).then_inc(F["params"], 1)

            def x1(hf):
                transposes((0, 5)[hf], tiles(XN, hf), F["x1T"], "x1", hf)

            def kq(hf):
                pe.wait_ge(ld["wkqv"], 48)
                pe.wait_ge(M["x1T_sb"], 2 * hf + 2)
                if hf == 1:
                    pe.wait_ge(M["vm_sb"], 3)
                pe.matmul(ps[:, (1, 6)[hf], :], wkqv[:, 0, :], XT[:, hf, :], start=True, stop=True).then_inc(F["k"], 1)
                pe.matmul(ps[:, (2, 7)[hf], :], wkqv[:, 1, :], XT[:, hf, :], start=True, stop=True).then_inc(F["q"], 1)

            def ctxT(hf):
                pe.wait_ge(ld["ctx"], 16)
                transposes(3 + hf, tiles(CX, hf), F["ctxT"])

            def values(c):
                pe.wait_ge(M["ctxT_sb"], c // 2 + 1)
                if c == 0:
                    pe.wait_ge(M["x1T_sb"], 4)
                if c == 2:
                    pe.wait_ge(M["params_sb"], 1)
                for b in range(4):
                    src = CT[:, c // 2, (4 * (c % 2) + b) * S:(4 * (c % 2) + b) * S + S]
                    for dup in range(2):
                        last = pe.matmul(ps[64 * dup:64 * dup + 64, (5, 6, 7, 3)[c], 128 * b:128 * b + 128], src,
                                         wkqv[:, 2, :], start=True, stop=True)
                last.then_inc(F["v"], 1)

            def lbT_():
                pe.wait_ge(ld["q"], 64)
                pe.wait_ge(M["k_sb"], 2)
                for n in range(6):
                    last = pe.transpose(ps[0:32, 5 + n // 4, 128 * (n % 4):128 * (n % 4) + 128], lb_sb[:, n, :], ident[:])
                last.then_inc(F["lbT"], 1)

            def weT_():
                pe.wait_ge(M["lbT_sb"], 1)
                pe.wait_ge(M["wdq_sb"], 1)
                for n in range(6):
                    o = ps[:, 5 + n // 4, 128 * (n % 4):128 * (n % 4) + 128]
                    pe.matmul(o, wdq[:, n, :], ident[:], start=True, stop=False)
                    last = pe.matmul(o, la_sb[:, n, :], lbT[:, n, :], start=False, stop=True)
                last.then_inc(F["weT"], 1)

            def k1(hf):
                pe.wait_ge(ld["l1"], 64)
                if hf == 0:
                    pe.wait_ge(M["q_sb"], 2)
                else:
                    pe.wait_ge(M["vn"], 1)
                tokens_out(7, CT[:, hf, :], wqkv1[:, 1, :], "k1")

            def v1(hf):
                pe.wait_ge(M["kn"], hf + 1)
                tokens_out(7, CT[:, hf, :], wqkv1[:, 2, :], "v1")

            def kv(hf, g):
                pe.wait_ge(M["kp_sb"], hf + 1)
                pe.wait_ge(M["vx_sb"], hf + 1)
                pe.wait_ge(M["vn"], 2)
                if (hf, g) != (0, 0):
                    pe.wait_ge(M["kvx_sb"], 4 * hf + g)
                for k, b in enumerate(kv_batches(hf, g)):
                    h0 = 64 * (b % 2)
                    last = pe.matmul(ps[:, 7, 132 * k:132 * k + 130], kp[h0:h0 + 64, b // 2, :],
                                     vx[h0:h0 + 64, b // 2, 0:130], start=True, stop=True)
                last.then_inc(F["kv"], 1)

            def S_(t):
                hf = t // HT
                if t == 0:
                    pe.wait_ge(consts, 1)
                pe.wait_ge(M["q_sb"], hf + 1)
                pe.wait_ge(M["keys_lo"], t + 1)
                pe.wait_ge(M["keys_hi"], t + 1)
                if t > 0:
                    pe.wait_ge(M["centered"], t)
                for hb in range(2):
                    pe.matmul(ps[:, hb, :], identb[:], causal[:].rearrange("p a s -> p (a s)"), start=True, stop=False)
                    for b in range(2):
                        tok = t * 128 + 64 * b
                        last = pe.matmul(ps[64 * b:64 * b + 64, hb, :], qT[:, hf, tok % HALF:tok % HALF + S],
                                         Km[:, t % 2, 8 * hb:8 * hb + 8, S * b:S * b + S], start=False, stop=True)
                last.then_inc(F["scores"], 1)

            def T1(t):
                pe.wait_ge(M["exped"], t + 1)
                for gq in range(2):
                    n = 2 * t + gq
                    if n >= 2:
                        pe.wait_ge(M["probsT_sb"], n - 1)
                    else:
                        pe.wait_ge(M["vm_sb"], 4)
                    for k in range(4):
                        pr = 4 * gq + k
                        last = pe.transpose(ps[:, 2 + gq, 128 * k:128 * k + 128],
                                            P[:, t % 2, 2 * pr:2 * pr + 2, :].rearrange("p a s -> p (a s)"), ident[:])
                    last.then_inc(F["probsT"], 1)

            def T2(t):
                pe.wait_ge(M["sums"], t + 1)
                if t > 0:
                    pe.wait_ge(M["heads_sb"], t)
                pe.transpose(ps[0:NH, 4, 0:128], rc[:, t % 2, :], ident[:]).then_inc(F["recT"], 1)

            def T3(t):
                pe.wait_ge(M["recT_sb"], t + 1)
                pe.matmul(ps[:, 4, 128:256], hmT[:], rT[:, t % 2, :], start=True, stop=True)
                pe.wait_ge(M["probsT_sb"], 2 * t + 2)
                for b in range(2):
                    for r in range(4):
                        last = pe.matmul(ps[32 * r:32 * r + 32, 4, 256 + 128 * b:384 + 128 * b],
                                         Vm[:, 2 * t + b, 32 * r:32 * r + 32],
                                         PT[:, t % 2, 2 * r:2 * r + 2, 64 * b:64 * b + 64], start=True, stop=True)
                last.then_inc(F["heads"], 1)

            def up(hf):
                pe.wait_ge(ld["mlp"], 32)
                pe.wait_ge(M["AT_sb"], 4 * hf + 4)
                if hf == 0:
                    pe.wait_ge(M["weT_sb"], 1)
                for j in range(4):
                    if j >= 2:
                        pe.wait_ge(M["up_sb"], 4 * hf + j - 1)
                    pe.matmul(ps[:, dbank(hf, j % 2), :], w1_sb[:, j, :], AT[:, hf, :], start=True, stop=True).then_inc(F["up"], 1)

            def down(hf):
                pe.wait_ge(M["up_sb"], 4 * hf + 4)
                pe.wait_ge(ld["rows_b"], 16 * 3)
                add_row(dbank(hf, 0), 0)
                for t in range(HT):
                    for j in range(4):
                        last = pe.matmul(ps[:, dbank(hf, 0), 128 * t:128 * t + 128], H1[:, j, 128 * t:128 * t + 128],
                                         w2_sb[:, j, :], start=False, stop=(j == 3 and t == HT - 1))
                last.then_inc(F["down"], 1)

            def x2T(hf):
                transposes(dbank(hf, 1), tiles(XN, hf), F["x2T"], "x2", hf)

            def y(hf, i):
                tokens_out(dbank(hf, i % 2), hT[:, hf, :], weT[:, 2 * i, :], "y", 1 + i,
                           ready="z_sb" if i else "x2T_sb", n=nth("z", hf, i - 1) if i else hf)

            def yT(hf, i):
                transposes(dbank(hf, 1 - i % 2), tiles(YN, hf), F["yT"], "yn", nth("yT", hf, i))

            def z(hf, i):
                n = nth("z", hf, i)
                if i < 2:
                    for u in range(2):
                        pe.wait_ge(M["gT_sb"], 2 * n + u + 1)
                        last = pe.matmul(ps[:, dbank(hf, i % 2), 256 * u:256 * u + 256], weT[:, 2 * i + 1, :],
                                         gT[:, hf, 256 * u:256 * u + 256], start=True, stop=True)
                    last.then_inc(F["z"], 1)
                else:
                    tokens_out(dbank(hf, 0), gT[:, hf, :], weT[:, 5, :], "z", 4, extra=[(hT[:, hf, :], ident[:])],
                               ready="gT_sb", n=n)

            def x3T(hf):
                transposes(dbank(hf, 1), tiles(XN, hf), F["x3T"], "x3", hf)

            def q1(hf):
                tokens_out(dbank(hf, 0), XT[:, hf, :], wqkv1[:, 0, :], "q1", ready="x3T_sb", n=hf)

            def q1T(hf):
                transposes(dbank(hf, 1), tiles(YN, hf), F["q1T"], "q1_read", hf)

            def att(hf):
                pe.wait_ge(M["kvx_sb"], 4 * hf + 4)
                for t in range(HT):
                    if t % 2 == 0:
                        pe.wait_ge(M["q1T_sb"], 2 * hf + t // 2 + 1)
                    for b in range(2):
                        last = pe.matmul(ps[64 * b:64 * b + 64, dbank(hf, t // 2), 144 * (t % 2):144 * (t % 2) + 144],
                                         qT[:, hf, 128 * t + 64 * b:128 * t + 64 * b + 64],
                                         kvx[:, 8 * hf + 2 * t + b, :], start=True, stop=True)
                last.then_inc(F["att"], 1)

            def hE_(hf):
                pe.wait_ge(M["att_sb"], hf + 1)
                for e in range(HD):
                    last = pe.transpose(ps[0:64, dbank(hf, e // 4), 128 * (e % 4):128 * (e % 4) + 128],
                                        AO[:, HT * hf:HT * hf + HT, e:D:HD], ident[:])
                last.then_inc(F["hE"], 1)

            def attT(hf):
                pe.wait_ge(M["hE_sb"], 2 * hf + 2)
                for m in range(8):
                    last = pe.transpose(ps[:, dbank(hf, 0), 64 * m:64 * m + 64], hE[:, hf, 16 * m:16 * m + 16, :], ident[0:64, 0:64])
                last.then_inc(F["attT"], 1)

            def dense(hf):
                pe.wait_ge(M["attT_sb"], hf + 1)
                tokens_out(dbank(hf, 1), AT[:, hf, :], dw_sb[:], "dense", 5)

            def x4T(hf):
                transposes(dbank(hf, 0), tiles(XN, hf), F["x4T"], "x4", hf)

            def gate(hf):
                for t in range(HT):
                    if t % 2 == 0:
                        pe.wait_ge(M["x4T_sb"], 2 * hf + t // 2 + 1)
                    last = pe.matmul(ps[:, dbank(hf, 1), 8 * t:8 * t + 8], XT[:, hf, 128 * t:128 * t + 128],
                                     PC[:, R_GATE:R_GATE + 8], start=True, stop=True)
                last.then_inc(F["gate"], 1)

            def chunk(c, slot, j, hf):
                k0, kn = KC[j]
                pe.wait_ge(M["act_sb"], c)
                for u in range(2):
                    mm = pe.matmul(ps[0:kn, PAIR[(slot + j) % 2][u], :], ew1[:, slot, u * INTER + k0:u * INTER + k0 + kn],
                                   XT[:, hf, :], start=True, stop=True)
                mm.then_inc(F["h"], 1)

            def products(slot, u):
                for t in (2 * u, 2 * u + 1):
                    for j, (k0, kn) in enumerate(KC):
                        last = pe.matmul(ps[:, 7, 128 * t:128 * t + 128], am[0:kn, slot, j, 128 * t:128 * t + 128],
                                         ew2[0:kn, slot, j, :], start=(j == 0), stop=(j == 2))
                return last

            def load_wait(r):
                return 16 * (r // 2 + 1)

            def C(c):
                r, j = c // 3, c % 3
                if c == 0:
                    pe.wait_ge(M["gate_read"], 1)
                    pe.wait_ge(M["kvx_sb"], 8)
                if j == 0:
                    pe.wait_ge(ld_w1[r % 2], load_wait(r))
                if c > 0:
                    chunk(c, r % 2, j, 0)
                else:
                    for u in range(2):
                        mm = pe.matmul(ps[:, PAIR[0][u], :], ew1[:, 0, u * INTER:u * INTER + 128], XT[:, 0, :], start=True, stop=True)
                    mm.then_inc(F["h"], 1)

            def P_(r, u):
                if u == 0:
                    pe.wait_ge(ld_w2[r % 2], 2 * load_wait(r))
                    pe.wait_ge(M["act_sb"], 3 * r + 4)
                    if r > 0:
                        pe.wait_ge(M["oe_read"], r)
                last = products(r % 2, u)
                if u == 1:
                    last.then_inc(F["oe"], 1)

            def later_round(r, slot, w1_loaded, w2_loaded):
                pe.wait_ge(ld_w1[slot], w1_loaded)
                chunk(3 * r, slot, 0, 1)
                pe.wait_ge(ld_w2[1 - slot], w2_loaded)
                pe.wait_ge(M["act_sb"], 3 * r + 1)
                pe.wait_ge(M["oe_read"], r - 1)
                products(1 - slot, 0)
                chunk(3 * r + 1, slot, 1, 1)
                products(1 - slot, 1).then_inc(F["oe"], 1)
                chunk(3 * r + 2, slot, 2, 1)

            def rounds():
                pe.wait_ge(M["x4T_sb"], 4)
                later_round(E, 0, load_wait(E), 2 * load_wait(E - 1))
                with pe.Fori(0, E // 2 - 1) as i:
                    later_round(2 * i + (E + 1), 1, 16 * i + load_wait(E + 1), 32 * i + 2 * load_wait(E))
                    later_round(2 * i + (E + 2), 0, 16 * i + load_wait(E + 2), 32 * i + 2 * load_wait(E + 1))
                later_round(2 * E - 1, 1, load_wait(2 * E - 1), 2 * load_wait(2 * E - 2))
                P_(2 * E - 1, 0)
                P_(2 * E - 1, 1)

            STEPS = dict(params=params, x1=x1, kq=kq, ctxT=ctxT, v=values, S=S_, T1=T1, T2=T2, T3=T3, lbT=lbT_, weT=weT_, k1=k1, v1=v1, kv=kv,
                         up=up, down=down, x2T=x2T, y=y, yT=yT, z=z, x3T=x3T, q1=q1, q1T=q1T, att=att, hE=hE_,
                         attT=attT, dense=dense, x4T=x4T, gate=gate, C=C, P=P_, rounds=rounds)
            for name, *args in ORDER:
                if name in STEPS:
                    STEPS[name](*args)

        @block.scalar
        def _(act):
            a = nc.scalar

            def evacuate(dst, src, want, count, done):
                act.wait_ge(F[want], count)
                a.copy(dst, src).then_inc(M[done], 1)

            def evacuate_halves(dst, bank, want, n, done):
                for u in range(2):
                    evacuate(dst[:, 256 * u:256 * u + 256], ps[:, bank, 256 * u:256 * u + 256], want, n + 1, done)

            def ctxT(hf):
                evacuate(CT[:, hf, :], ps[:, 3 + hf, :], "ctxT", hf + 1, "ctxT_sb")

            def x1(hf):
                evacuate_halves(XT[:, hf, :], (0, 5)[hf], "x1T", hf, "x1T_sb")

            def kq(hf):
                act.wait_ge(M["params_sb"], 1)
                act.wait_ge(F["k"], hf + 1)
                a.activation(kT[:, hf, :], ps[:, (1, 6)[hf], :], ACT.Identity, bias=PC[:, R_BK:R_BK + 1]).then_inc(M["k_sb"], 1)
                act.wait_ge(F["q"], hf + 1)
                a.activation(qT[:, hf, :], ps[:, (2, 7)[hf], :], ACT.Identity, bias=PC[:, R_BQ:R_BQ + 1]).then_inc(M["q_sb"], 1)

            def fold(dst, src, want, done):
                act.wait_ge(F[want], 1)
                a.copy(dst[:, 0:4, :].rearrange("p n d -> p (n d)"), src[:, 5, :])
                a.copy(dst[:, 4:6, :].rearrange("p n d -> p (n d)"), src[:, 6, 0:256]).then_inc(M[done], 1)

            def lbT_():
                fold(lbT, ps[0:32], "lbT", "lbT_sb")

            def weT_():
                fold(weT, ps, "weT", "weT_sb")

            def S_(t):
                act.wait_ge(M["centered"], t + 1)
                a.activation(P[:, t % 2], P[:, t % 2], ACT.Exp).then_inc(M["exped"], 1)

            def T1(t):
                for gq in range(2):
                    n = 2 * t + gq
                    if t > 1:
                        act.wait_ge(F["heads"], t - 1)
                    evacuate(PT[:, t % 2, 4 * gq:4 * gq + 4, :].rearrange("p n q -> p (n q)"), ps[:, 2 + gq, :],
                             "probsT", n + 1, "probsT_sb")

            def T3(t):
                act.wait_ge(M["heads_sb"], t + 1)
                a.activation(AT[:, t // HT, 128 * (t % HT):128 * (t % HT) + 128], o2[:, t % 2].rearrange("p b s -> p (b s)"),
                             ACT.Identity, bias=PC[:, R_BV:R_BV + 1]).then_inc(M["AT_sb"], 1)

            def up(hf):
                if hf == 1:
                    act.wait_ge(F["down"], 1)
                for j in range(4):
                    act.wait_ge(F["up"], 4 * hf + j + 1)
                    a.activation(H1[:, j, :], ps[:, dbank(hf, j % 2), :], ACT.Gelu,
                                 bias=PC[:, R_B1 + j:R_B1 + j + 1]).then_inc(M["up_sb"], 1)

            def down(hf):
                if hf == 0:
                    act.wait_ge(ld["gates"], 32)
                    a.activation(tg[:], gts[:], ACT.Tanh).then_inc(M["tanh_sb"], 1)

            def x2T(hf):
                evacuate_halves(hT[:, hf, :], dbank(hf, 1), "x2T", hf, "x2T_sb")

            def yT(hf, i):
                act.wait_ge(F["yT"], nth("yT", hf, i) + 1)
                for u in range(2):
                    h_ = slice(256 * u, 256 * u + 256)
                    a.activation(gT[:, hf, h_], ps[:, dbank(hf, 1 - i % 2), h_], ACT.Gelu, bias=PC[:, R_FBETA + i:R_FBETA + i + 1],
                                 scale=PC[:, R_FG + i:R_FG + i + 1]).then_inc(M["gT_sb"], 1)

            def x3T(hf):
                evacuate_halves(XT[:, hf, :], dbank(hf, 1), "x3T", hf, "x3T_sb")

            def q1T(hf):
                act.wait_ge(F["q1T"], hf + 1)
                for u in range(2):
                    h_ = slice(256 * u, 256 * u + 256)
                    a.activation(kT[:, hf, h_], ps[:, dbank(hf, 1), h_], ACT.Relu, bias=PC[:, R_LB:R_LB + 1],
                                 scale=PC[:, R_LG:R_LG + 1]).then_inc(M["relu_sb"], 1)

            def hE_(hf):
                act.wait_ge(F["hE"], hf + 1)
                for u in range(2):
                    a.copy(hE[:, hf, :, 4 * u:4 * u + 4].rearrange("p n e -> p e n"),
                           ps[0:64, dbank(hf, u), :].rearrange("p (e n) -> p e n", e=4)).then_inc(M["hE_sb"], 1)

            def attT(hf):
                act.wait_ge(F["attT"], hf + 1)
                for b in range(2):
                    last = a.copy(AT[:, hf, :].rearrange("c (t b h q) -> c b q t h", t=HT, b=2, h=NH)[:, b],
                                  ps[:, dbank(hf, 0), 256 * b:256 * b + 256].rearrange("c (q t h) -> c q t h", q=4, t=HT))
                last.then_inc(M["attT_sb"], 1)

            def x4T(hf):
                evacuate_halves(XT[:, hf, :], dbank(hf, 0), "x4T", hf, "x4T_sb")

            def route(hf):
                act.wait_ge(M["dlog"], hf + 1)
                a.activation(el[:, HT * hf:HT * hf + HT], dl[:, HT * hf:HT * hf + HT], ACT.Exp).then_inc(M["el_sb"], 1)

            def silu(c, par_, j, first=False):
                kn = KC[j][1]
                act.wait_ge(F["h"], c + 1)
                if not first:
                    act.wait_ge(M["act_sb"], c)
                a.activation(sg[0:kn, par_, :], ps[0:kn, PAIR[par_][0], :], ACT.Silu).then_inc(M["silu"], 1)

            def C(c):
                silu(c, c % 2, c % 3, c == 0)

            def rounds():
                with act.Fori(0, E // 2) as i:
                    for slot in range(2):
                        for j in range(3):
                            silu(6 * i + (3 * E + 3 * slot + j), (3 * slot + j) % 2, j)

            STEPS = dict(ctxT=ctxT, x1=x1, kq=kq, lbT=lbT_, weT=weT_, M=S_, T1=T1, T3=T3, up=up, down=down, x2T=x2T, yT=yT, x3T=x3T,
                         q1T=q1T, hE=hE_, attT=attT, x4T=x4T, route=route, C=C, rounds=rounds)
            for name, *args in ORDER:
                if name in STEPS:
                    STEPS[name](*args)

        @block.vector
        def _(dve):
            v = nc.vector
            n = [0]
            ln = [0]

            def link(ins):
                n[0] += 1
                ins.then_inc(dve_step, 1)
                dve.wait_ge(dve_step, n[0])

            def stats(src, filled=None, n=0):
                if filled is not None:
                    dve.wait_ge(F[filled], n + 1)
                for t in range(HT):
                    ins = v.bn_stats(bst[:, t, :], src[:, t, :])
                link(ins)
                for t in range(HT):
                    ins = v.bn_aggr(mv[:, ln[0], t, :], bst[:, t, :])
                ins.then_inc(M["ln_var"], 1)
                ln[0] += 1
                dve.wait_ge(M["ln_var"], ln[0])
                return ln[0] - 1

            def normalize(i, src, dst, done, halves=True):
                dve.wait_ge(M["ln_rstd"], i + 1)
                for t in range(HT):
                    ins = v.tensor_scalar(dst[:, t, :], src[:, t, :], mv[:, i, t, 0:1], rstd[:, i, t:t + 1],
                                          ALU.subtract, ALU.mult)
                    if t == HT - 1 or (halves and t == 1):
                        ins.then_inc(M[done], 1)

            def tiles(t, hf):
                return t[:, HT * hf:HT * hf + HT, :]

            def flat(t, hf):
                return tiles(t, hf).rearrange("p t d -> p (t d)")

            def bank(b):
                return ps[:, b, :].rearrange("p (t d) -> p t d", t=HT)

            ids = {}

            def params():
                v.engine_nop().then_inc(M["act_sb"], 1)
                dve.wait_ge(F["params"], 1)
                v.tensor_copy(PC[:], ps[:, 7, 0:R_END]).then_inc(M["params_sb"], 1)

            def x1(hf):
                dve.wait_ge(ld_x[hf], 16)
                i = stats(tiles(X, hf))
                normalize(i, tiles(X, hf), tiles(XN, hf), "x1")

            def K(t):
                if t == 0:
                    dve.wait_ge(hm_ready, 1)
                place_keys(dve, v, t, 0)

            def values(c):
                if c == 0:
                    dve.wait_ge(consts, 1)
                dve.wait_ge(F["v"], c + 1)
                v.tensor_tensor(Vm[:, 4 * c:4 * c + 4, :], ps[:, (5, 6, 7, 3)[c], :].rearrange("p (b d) -> p b d", b=4),
                                par[:].rearrange("p h d -> p (h d)").unsqueeze(1).to_broadcast([128, 4, 128]),
                                ALU.mult).then_inc(M["vm_sb"], 1)
                if c == 3:
                    v.tensor_copy(blk[:], hm[:].unsqueeze(2).to_broadcast([128, NH, HD]))
                    link(v.tensor_reduce(pairsel[:, 0:2], hm[:].rearrange("p (r s j) -> p s r j", r=4, s=2), axis=AX.XY, op=ALU.add))

            def weights():
                dve.wait_ge(ld["q"], 64)
                link(v.tensor_copy(wf, qw_sb[:]))
                link(v.tensor_scalar(wf, wf, 1.0 / 7.5, -1.0, ALU.mult, ALU.add))
                v.tensor_tensor(wdq[:].rearrange("p n (g k) -> p (n g) k", g=8),
                                wf.rearrange("p n (g k) -> p (n g) k", g=8),
                                sc_sb[:].rearrange("p n g -> p (n g)").unsqueeze(2).to_broadcast([128, 48, 16]),
                                ALU.mult).then_inc(M["wdq_sb"], 1)

            def k1(hf):
                ids["k", hf] = stats(bank(7), "k1", hf)

            def k1n(hf):
                normalize(ids["k", hf], bank(7), tiles(kn, hf), "kn", halves=False)

            def v1(hf):
                ids["v", hf] = stats(bank(7), "v1", hf)

            def v1n(hf):
                normalize(ids["v", hf], bank(7), tiles(vn, hf), "vn", halves=False)

            def kv(hf, g):
                dve.wait_ge(F["kv"], 4 * hf + g + 1)
                bs = kv_batches(hf, g)
                nb = len(bs)
                kvb = ps[:, 7, 0:132 * nb].rearrange("p (b d) -> p b d", b=nb)
                v.tensor_tensor(kvx[:, bs[0]:bs[-1] + 1:2, 0:D], kvb[:, :, 0:D],
                                blk[:].rearrange("p h d -> p (h d)").unsqueeze(1).to_broadcast([128, nb, D]), ALU.mult)
                for b in range(nb):
                    ins = v.tensor_scalar(kvx[:, bs[b], D:D + NH], hm[:], kvb[:, b, D:D + 1], None, ALU.mult)
                ins.then_inc(M["kvx_sb"], 1)

            def S_(t):
                sc = ps[:, 0:2, :].rearrange("p u (h s) -> p (u h) s", s=S)
                dve.wait_ge(F["scores"], t + 1)
                link(v.tensor_reduce(mx[:, t % 2, :], sc, axis=AX.X, op=ALU.max))
                if t > 1:
                    dve.wait_ge(F["probsT"], 2 * t - 2)
                    dve.wait_ge(M["sums"], t - 1)
                v.tensor_tensor(P[:, t % 2], sc, mx[:, t % 2, :].unsqueeze(2).to_broadcast([128, NH, S]),
                                ALU.subtract).then_inc(M["centered"], 1)

            def T1(t):
                s = t % 2
                dve.wait_ge(M["exped"], t + 1)
                link(v.tensor_reduce(sm[:, s, :], P[:, s], axis=AX.X, op=ALU.add))
                if t > 1:
                    dve.wait_ge(F["recT"], t - 1)
                v.reciprocal(rc[:, s, :], sm[:, s, :]).then_inc(M["sums"], 1)

            def T2(t):
                s = t % 2
                dve.wait_ge(F["recT"], t + 1)
                v.tensor_copy(rT[:, s, :], ps[0:NH, 4, 0:128]).then_inc(M["recT_sb"], 1)

            def T3(t):
                s = t % 2
                dve.wait_ge(F["heads"], t + 1)
                if t > 1:
                    dve.wait_ge(M["AT_sb"], t - 1)
                    dve.wait_ge(M["heads_sb"], t - 1)
                ob = ps[:, 4, 256:512].rearrange("p (b j q) -> p b j q", b=2, j=2)
                link(v.tensor_scalar(o0[:, s], ob[:, :, 0, :], pairsel[:, 0:1], None, ALU.mult))
                link(v.scalar_tensor_tensor(o1[:, s], ob[:, :, 1, :], pairsel[:, 1:2], o0[:, s], ALU.mult, ALU.add))
                v.tensor_tensor(o2[:, s].rearrange("p b s -> p (b s)"), o1[:, s].rearrange("p b s -> p (b s)"),
                                ps[:, 4, 128:256], ALU.mult).then_inc(M["heads_sb"], 1)

            def add_gated(g, b, hf, filled, n):
                dve.wait_ge(F[filled], n + 1)
                return v.scalar_tensor_tensor(flat(X, hf), ps[:, b, :], tg[:, g:g + 1], flat(X, hf), ALU.mult, ALU.add)

            def down(hf):
                dve.wait_ge(M["tanh_sb"], 1)
                link(add_gated(0, dbank(hf, 0), hf, "down", hf))
                ids[hf] = stats(tiles(X, hf))

            def x2T(hf):
                normalize(ids[hf], tiles(X, hf), tiles(XN, hf), "x2")

            def y(hf, i):
                ids[hf] = stats(bank(dbank(hf, i % 2)), "y", nth("y", hf, i))

            def yT(hf, i):
                normalize(ids[hf], bank(dbank(hf, i % 2)), tiles(YN, hf), "yn")

            def z(hf, i):
                n = nth("z", hf, i)
                if i < 2:
                    dve.wait_ge(F["z"], n + 1)
                    for u in range(2):
                        h_ = slice(256 * u, 256 * u + 256)
                        v.scalar_tensor_tensor(hT[:, hf, h_], ps[:, dbank(hf, i % 2), h_], PC[:, R_FB + 2 * i + 1:R_FB + 2 * i + 2],
                                               hT[:, hf, h_], ALU.add, ALU.add).then_inc(M["z_sb"], 1)
                else:
                    add_gated(2, dbank(hf, 0), hf, "z", n).then_inc(M["z_sb"], 2)
                    dve.wait_ge(M["z_sb"], 2 * n + 2)
                    ids[hf] = stats(tiles(X, hf))

            def x3T(hf):
                normalize(ids[hf], tiles(X, hf), tiles(XN, hf), "x3")

            def q1(hf):
                ids[hf] = stats(bank(dbank(hf, 0)), "q1", hf)

            def q1T(hf):
                normalize(ids[hf], bank(dbank(hf, 0)), tiles(YN, hf), "q1_read")

            def q1e(hf):
                for u in range(2):
                    h_ = slice(256 * u, 256 * u + 256)
                    dve.wait_ge(M["relu_sb"], 2 * hf + u + 1)
                    v.tensor_scalar(qT[:, hf, h_], kT[:, hf, h_], 1e-6, None, ALU.add).then_inc(M["q1T_sb"], 1)

            def att(hf):
                dve.wait_ge(F["att"], hf + 1)
                for u in range(2):
                    z_ = zz[:, 2 * hf + u]
                    av = ps[:, dbank(hf, u), 0:288].rearrange("p (t c) -> p t c", t=2)
                    link(v.tensor_scalar(z_, av[:, :, D:D + NH], 1e-6, None, ALU.add))
                    link(v.reciprocal(z_, z_))
                    ins = v.tensor_tensor(AO[:, HT * hf + 2 * u:HT * hf + 2 * u + 2, :].rearrange("p t (h d) -> p t h d", h=NH),
                                          av[:, :, 0:D].rearrange("p t (h d) -> p t h d", h=NH),
                                          z_.unsqueeze(3).to_broadcast([128, 2, NH, HD]), ALU.mult)
                ins.then_inc(M["att_sb"], 1)

            def dense(hf):
                i = ids[hf] = stats(bank(dbank(hf, 1)), "dense", hf)
                if hf == 0:
                    dve.wait_ge(M["xb"], 1)
                for t in range(HT):
                    ins = v.scalar_tensor_tensor(YN[:, HT * hf + t, :], ps[:, dbank(hf, 1), 128 * t:128 * t + 128],
                                                 mv[:, i, t, 0:1], gated_gb[:, 0, :], ALU.subtract, ALU.mult)
                ins.then_inc(M["dense_read"], 1)

            def X3(hf):
                dve.wait_ge(M["ln_rstd"], ids[hf] + 1)
                dve.wait_ge(M["xb"], hf + 1)
                dve.wait_ge(M["dense_read"], hf + 1)
                for t in range(HT * hf, HT * hf + HT):
                    ins = v.scalar_tensor_tensor(X[:, t, :], YN[:, t, :], rstd[:, ids[hf], t % HT:t % HT + 1], XB[:, t, :],
                                                 ALU.mult, ALU.add)
                link(ins)
                ids[hf] = stats(tiles(X, hf))

            def x4T(hf):
                normalize(ids[hf], tiles(X, hf), tiles(XN, hf), "x4")

            def gate(hf):
                dve.wait_ge(F["gate"], hf + 1)
                v.tensor_copy(tiles(lg, hf), ps[:, dbank(hf, 1), 0:32].rearrange("p (t e) -> p t e", t=HT)).then_inc(M["gate_read"], 1)
                dve.wait_ge(M["gate_read"], hf + 1)
                ts = range(HT * hf, HT * hf + HT)
                for t in ts:
                    ins = v.max(top[:, t, :], lg[:, t, :])
                link(ins)
                h_ = slice(HT * hf, HT * hf + HT)
                v.tensor_tensor(dl[:, h_], top[:, h_, 1], top[:, h_, 0], ALU.subtract).then_inc(M["dlog"], 1)
                for t in ts:
                    ins = v.max_index(topi[:, t, :], top[:, t, :], lg[:, t, :])
                link(ins)
                link(v.tensor_copy(topf[:, h_, :], topi[:, h_, :]))

            def route(hf):
                h_ = slice(HT * hf, HT * hf + HT)
                dve.wait_ge(M["el_sb"], hf + 1)
                link(v.tensor_scalar(den[:, h_], el[:, h_], 1.0, None, ALU.add))
                link(v.reciprocal(tw[:, h_, 0], den[:, h_]))
                link(v.tensor_tensor(tw[:, h_, 1], tw[:, h_, 0], el[:, h_], ALU.mult))
                link(v.tensor_scalar(tw[:, h_, :], tw[:, h_, :], tg[:, 3:4], None, ALU.mult))
                for s in range(2):
                    link(v.tensor_tensor(oh[:, h_, s, :], iota8[:].unsqueeze(1).to_broadcast([128, HT, 8]),
                                         topf[:, h_, s:s + 1].to_broadcast([128, HT, 8]), ALU.is_equal))
                    link(v.tensor_tensor(oh[:, h_, s, :], oh[:, h_, s, :], tw[:, h_, s:s + 1].to_broadcast([128, HT, 8]), ALU.mult))
                link(v.tensor_tensor(wexp[:, h_, :], oh[:, h_, 0, :], oh[:, h_, 1, :], ALU.add))

            def gated(c, slot, j, par_):
                kn = KC[j][1]
                dve.wait_ge(M["silu"], c + 1)
                v.tensor_tensor(am[0:kn, slot, j, :], ps[0:kn, PAIR[par_][1], :], sg[0:kn, par_, :], ALU.mult).then_inc(M["act_sb"], 1)

            def add_round(r, slot, hf, first=False):
                dve.wait_ge(F["oe"], r + 1)
                if not first:
                    dve.wait_ge(M["oe_read"], r)
                for t in range(HT):
                    ins = v.scalar_tensor_tensor(X[:, HT * hf + t, :], ps[:, 7, 128 * t:128 * t + 128],
                                                 wcur[:, slot, t:t + 1], X[:, HT * hf + t, :], ALU.mult, ALU.add)
                ins.then_inc(M["oe_read"], 1)

            def G(c):
                r, j = c // 3, c % 3
                if j == 0:
                    if r >= 2:
                        dve.wait_ge(F["oe"], r - 1)
                        dve.wait_ge(M["oe_read"], r - 1)
                    v.tensor_copy(wcur[:, r % 2, :], wexp[:, 0:HT, r])
                gated(c, r % 2, j, c % 2)

            def A(r):
                add_round(r, r % 2, 0, r == 0)

            def later_round(r, slot, weights, hf):
                dve.wait_ge(F["oe"], r - 1)
                dve.wait_ge(M["oe_read"], r - 1)
                v.tensor_copy(wcur[:, slot, :].unsqueeze(2), weights)
                gated(3 * r, slot, 0, slot)
                gated(3 * r + 1, slot, 1, 1 - slot)
                add_round(r - 1, 1 - slot, hf)
                gated(3 * r + 2, slot, 2, slot)

            def rounds():
                later_round(E, 0, wexp[:, HT:T, 0:1], 0)
                with dve.Fori(0, E // 2 - 1) as i:
                    for k in range(2):
                        later_round(2 * i + (E + 1 + k), 1 - k, wexp[:, HT:T, bass.ds(2 * i + (1 + k), 1)], 1)
                later_round(2 * E - 1, 1, wexp[:, HT:T, E - 1:E], 1)
                add_round(2 * E - 1, 1, 1)

            STEPS = dict(params=params, x1=x1, v=values, weights=weights, k1=k1, v1=v1, k1n=k1n, v1n=v1n, kv=kv, M=S_, K=K, T1=T1, T2=T2, T3=T3, q1e=q1e, down=down, x2T=x2T,
                         y=y, yT=yT, z=z, x3T=x3T, q1=q1, q1T=q1T, att=att, dense=dense, X3=X3, x4T=x4T, gate=gate,
                         route=route, G=G, A=A, rounds=rounds)
            for name, *args in ORDER:
                if name in STEPS:
                    STEPS[name](*args)


_INS = ['x', 'ctx_1024', 'mask_BxS2_ff1', 'g_xattn', 'g_ffn', 'L0_xattn_Wk', 'L0_xattn_bk', 'L0_xattn_Wq', 'L0_xattn_bq',
        'L0_xattn_Wv', 'L0_xattn_bv', 'L0_xattn_W1', 'L0_xattn_b1', 'L0_xattn_W2', 'L0_xattn_b2', 'L0_ffn_qweights',
        'L0_ffn_scales', 'L0_ffn_biases', 'L0_ffn_lora_a', 'L0_ffn_lora_b', 'L0_ffn_ln_gamma', 'L0_ffn_ln_beta',
        'L1_xattn_wq', 'L1_xattn_wk', 'L1_xattn_wv', 'L1_xattn_ln_gamma', 'L1_xattn_ln_beta', 'L1_xattn_dense_w',
        'L1_xattn_dense_b', 'L1_ffn_gate_w', 'L1_ffn_w1_stacked', 'L1_ffn_w2_stacked']


def kernel(**inputs):
    import numpy as _np
    import concourse.bacc as _bacc
    from concourse import mybir as _mybir
    from concourse.bass_utils import run_bass_kernel_spmd as _run

    nc = _bacc.Bacc("TRN2", target_bir_lowering=False, num_devices=1)
    arrays, args = {}, []
    for name in _INS:
        a = _np.ascontiguousarray(inputs[name])
        arrays[f"in_{name}_dram"] = a
        args.append(nc.dram_tensor(f"in_{name}_dram", a.shape, _mybir.dt.from_np(a.dtype), kind="ExternalInput").ap())
    out = nc.dram_tensor("out_0_dram", (16, 64, 128), _mybir.dt.float32, kind="ExternalOutput").ap()
    flamingo(nc, *args, out)
    r = _run(nc, [arrays], core_ids=[0])
    return r.results[0]["out_0_dram"]
```
